# Optimizing a Trainium2 kernel written in Bass

```python
import numpy as np
import jax
import jax.numpy as jnp

def _softmax(x, axis=-1):
    return jax.nn.softmax(x, axis=axis)

def _gelu(x):
    return jax.nn.gelu(x, approximate=True)

def _silu(x):
    return jax.nn.silu(x)

def _sigmoid(x):
    return jax.nn.sigmoid(x)

def _layernorm(x, axis=-1, eps=1e-05):
    m = jnp.mean(x, axis=axis, keepdims=True)
    v = jnp.var(x, axis=axis, keepdims=True)
    return (x - m) / jnp.sqrt(v + eps)

def _scatter_add(tgt, idx, src, axis=0):
    return tgt.at[idx].add(src)

def _segment_sum(src, seg, n):
    return jax.ops.segment_sum(src, seg, n)
kernel_name = 'mk_gnn_resnorm_d1_gnn_r32_19520d'

def setup_inputs(seed: int=0):
    np.random.seed(seed)
    _w = jnp.asarray

    def _rec_inputs():
        import jax
        import jax.numpy as jnp
        _gk = jax.random.key(seed)
        x = -0.0008691 + 1 * jax.random.normal(jax.random.fold_in(_gk, 1), (3125, 64), jnp.float32)
        _s = jax.random.randint(jax.random.fold_in(_gk, 2), (25000,), 0, 3125, jnp.int32)
        _d = jax.random.randint(jax.random.fold_in(_gk, 3), (25000,), 0, 3125, jnp.int32)
        _loop = jnp.arange(3125, dtype=jnp.int32)
        src = jnp.concatenate([_s, _d, _loop])
        dst = jnp.concatenate([_d, _s, _loop])
        _o = jnp.argsort(dst, stable=True)
        src = src[_o]
        dst = dst[_o]
        edge_attr_8 = -0.000153872 + 1.00011 * jax.random.normal(jax.random.fold_in(_gk, 12), (53125, 8), jnp.float32)
        return (x, src, dst, edge_attr_8)
    x, src, dst, edge_attr_8 = _rec_inputs()

    def _L0_gnn_setup():
        import jax, jax.numpy as jnp
        import numpy as np
        N_NODES = 625
        N_EDGES = 31250
        C = 64
        H = 64
        N_BASIS = 8
        key = jax.random.key(seed)
        ks = jax.random.split(key, 10)

        def glorot(k, shape):
            fan_in, fan_out = (shape[0], shape[1])
            lim = np.sqrt(6.0 / (fan_in + fan_out)).astype(np.float32)
            return jax.random.uniform(k, shape, jnp.float32, -lim, lim)
        return {'p': jax.random.normal(ks[0], (N_NODES, C), jnp.float32), 'idx_i': jax.random.randint(ks[1], (N_EDGES,), 0, N_NODES), 'idx_j': jax.random.randint(ks[2], (N_EDGES,), 0, N_NODES), 'basis': jax.random.normal(ks[3], (N_EDGES, N_BASIS), jnp.float32), 'pp_W': glorot(ks[4], (C, C)), 'pp_b': jnp.zeros((C,), jnp.float32), 'pi_W1': glorot(ks[5], (2 * C, H)), 'pi_b1': jnp.zeros((H,), jnp.float32), 'pi_W2': glorot(ks[6], (H, H * N_BASIS)), 'ii_W': glorot(ks[7], (H, C)), 'ii_b': jnp.zeros((C,), jnp.float32)}
    _L0_gnn_all = _L0_gnn_setup()
    _L0_gnn_in = {k: v for k, v in _L0_gnn_all.items() if k in ('pp_W', 'pp_b', 'pi_W1', 'pi_b1', 'pi_W2', 'ii_W', 'ii_b')}
    del _L0_gnn_all
    return {'x': x, 'src': src, 'dst': dst, 'edge_attr_8': edge_attr_8, 'L0_gnn_pp_W': _L0_gnn_in['pp_W'], 'L0_gnn_pp_b': _L0_gnn_in['pp_b'], 'L0_gnn_pi_W1': _L0_gnn_in['pi_W1'], 'L0_gnn_pi_b1': _L0_gnn_in['pi_b1'], 'L0_gnn_pi_W2': _L0_gnn_in['pi_W2'], 'L0_gnn_ii_W': _L0_gnn_in['ii_W'], 'L0_gnn_ii_b': _L0_gnn_in['ii_b']}

def reference(x, src, dst, edge_attr_8, L0_gnn_pp_W, L0_gnn_pp_b, L0_gnn_pi_W1, L0_gnn_pi_b1, L0_gnn_pi_W2, L0_gnn_ii_W, L0_gnn_ii_b):
    import jax
    import jax.numpy as jnp

    def _L0_gnn_ref(p, idx_i, idx_j, basis, pp_W, pp_b, pi_W1, pi_b1, pi_W2, ii_W, ii_b):
        import jax, jax.numpy as jnp
        import numpy as np
        N_NODES = 625
        N_EDGES = 31250
        C = 64
        H = 64
        N_BASIS = 8
        p1 = jnp.tanh(p @ pp_W + pp_b)
        pair = jnp.concatenate([p1[idx_i], p1[idx_j]], axis=-1)
        h = pair @ pi_W1 + pi_b1
        h = (h @ pi_W2).reshape(-1, H, N_BASIS)
        i1 = jnp.einsum('ecb,eb->ec', h, basis)
        i2 = jnp.tanh(i1 @ ii_W + ii_b)
        return p.at[idx_i].add(i2)
    x = _layernorm(x + _L0_gnn_ref(x, src, dst, edge_attr_8, L0_gnn_pp_W, L0_gnn_pp_b, L0_gnn_pi_W1, L0_gnn_pi_b1, L0_gnn_pi_W2, L0_gnn_ii_W, L0_gnn_ii_b), axis=-1)
    return x

_drawn_inputs = setup_inputs


def setup_inputs(seed=0):
    import zlib

    import numpy as np

    out = dict(_drawn_inputs(seed))
    spreads = {'L0_gnn_pp_b': (0.0, 0.1), 'L0_gnn_pi_b1': (0.0, 0.1), 'L0_gnn_ii_b': (0.0, 0.1)}
    factors = {}
    for name, (base, spread) in spreads.items():
        noise = np.random.default_rng([zlib.crc32(name.encode()), seed]).standard_normal(out[name].shape)
        drawn = base * np.exp(spread * noise) if base else spread * noise
        out[name] = jnp.asarray(drawn.astype(out[name].dtype))
    for name, factor in factors.items():
        out[name] = (out[name] * factor).astype(out[name].dtype)
    return out
```

```python
import concourse.bass as bass
from concourse import mybir
from contextlib import ExitStack

F32 = mybir.dt.float32
F16 = mybir.dt.float16
BF16 = mybir.dt.bfloat16
I32 = mybir.dt.int32
U32 = mybir.dt.uint32
ALU = mybir.AluOpType
ACT = mybir.ActivationFunctionType
AX = mybir.AxisListType


def gnn_residual_norm_kernel(nc, x, src, dst, basis, pp_w, pp_b, pi_w1, pi_b1, pi_w2, ii_w, ii_b, out):
    P = 128
    N, C = x.shape
    E = src.shape[0]
    NB = basis.shape[1]
    H = ii_w.shape[0]
    CH = NB * H // P
    EPP = E // P
    TAIL = E - P * EPP
    TG = 4
    TILES = EPP + 1
    GROUPS = TILES // TG
    assert TILES % (2 * TG) == 0 and TAIL <= P and C == H == 64
    HALF = (N + 1) // 2 + 1
    REST = N - HALF
    SB_COLS = HALF // 4
    assert HALF % 4 == 0 and SB_COLS <= 512
    FULL = HALF // P
    BLK = FULL + 1
    HTAIL = (HALF - FULL * P, REST - FULL * P)

    a_table = nc.dram_tensor("a_table", (N, H), F32, kind="Internal").ap()
    b_table = nc.dram_tensor("b_table", (N, H), F32, kind="Internal").ap()

    ctx = ExitStack()
    with ctx:
        def sb(name, shape, dt=F32):
            return ctx.enter_context(nc.sbuf_tensor(name, shape, dt))

        def sem(name):
            return ctx.enter_context(nc.semaphore(name))

        bank = [ctx.enter_context(nc.psum_tensor(f"bank{i}", [P, 512], F32)) for i in range(8)]
        sums_ps = bank[0:4]
        turn_ps = bank[4:6]
        z_ps = bank[6:8]

        index = sb("index", [P, 2, TILES], I32)
        basis_sb = sb("basis_sb", [P, TILES, NB])
        x_sb = sb("x_sb", [P, BLK, 2, C])
        w_diag = sb("w_diag", [P, 2, C])
        w1_diag = sb("w1_diag", [P, 2, 2, H])
        b1_row = sb("b1_row", [P, 2, 2, H])
        ppb_col = sb("ppb_col", [P, 1])
        w2_sb = sb("w2_sb", [H, H * NB])
        iiw_sb = sb("iiw_sb", [H, C])
        iib3 = sb("iib3", [3, C])
        ident = sb("ident", [P, P])
        node_i = sb("node_i", [P, HALF], I32)
        node_row = sb("node_row", [P, HALF], F16)
        x_turned = sb("x_turned", [P, BLK * P])
        p1_turned = sb("p1_turned", [P, BLK * P])
        ab_sb = sb("ab_sb", [P, BLK, 2, 2, H])
        w2_turned = sb("w2_turned", [H, NB, H])
        v_sb = sb("v_sb", [P, CH, C])
        bias_parts = sb("bias_parts", [3, 3, C])
        bias_left = sb("bias_left", [3, 2, C])
        bias_b16 = sb("bias_b16", [3, C], BF16)
        bias_mix = sb("bias_mix", [3, 2, C])
        bias3 = sb("bias3", [3, TG, C], BF16)
        ones3 = sb("ones3", [3, P], BF16)
        zeros = sb("zeros", [P, 512], BF16)
        src_f = sb("src_f", [P, TILES])
        row_f = sb("row_f", [P, TILES])
        upper = sb("upper", [P, TILES])
        mask = sb("mask", [P, TILES, 2], F16)
        stage = sb("stage", [P, 2, 2, TG], I32)
        rows = sb("rows", [P, 2, 2, TG, H])
        h_sb = sb("h_sb", [P, 2, TG, H])
        weighted = sb("weighted", [P, 2, TG, NB, H])
        turned = sb("turned", [P, TG, CH, P])
        msg = sb("msg", [P, 2, TG, C])
        split = sb("split", [P, 2, 2, TG, C], F16)
        parts = sb("parts", [P, 2, 2, TG, 2, C], F16)
        onehot = sb("onehot", [P, 2, TG, HALF], F16)
        agg = sb("agg", [P, HALF])
        y = sb("y", [P, BLK, 2, C])
        sq = sb("sq", [P, BLK, 2, C])
        mean = sb("mean", [P, BLK, 2])
        var = sb("var", [P, BLK, 2])
        std = sb("std", [P, BLK, 2])
        rstd = sb("rstd", [P, BLK, 2])
        eps = sb("eps", [P, 1])

        s_edges = sem("s_edges")
        s_x = sem("s_x")
        s_w = sem("s_w")
        s_w2 = sem("s_w2")
        s_pre = sem("s_pre")
        s_ident = sem("s_ident")
        s_iota = sem("s_iota")
        s_dve = sem("s_dve")
        s_xt = sem("s_xt")
        s_xc = sem("s_xc")
        s_p1 = sem("s_p1")
        s_th = sem("s_th")
        s_ab = sem("s_ab")
        s_abc = sem("s_abc")
        s_w2t = sem("s_w2t")
        s_w2c = sem("s_w2c")
        s_v = sem("s_v")
        s_vc = sem("s_vc")
        s_bias = sem("s_bias")
        s_tables = sem("s_tables")
        staged = sem("staged")
        pool_turns = sem("pool_turns")
        gathered = [sem("gathered0"), sem("gathered1")]
        h_added = sem("h_added")
        weighed = sem("weighed")
        transposed = sem("transposed")
        copied = sem("copied")
        projected = sem("projected")
        activated = sem("activated")
        rest_ready = sem("rest_ready")
        parts_ready = sem("parts_ready")
        onehot_ready = sem("onehot_ready")
        scattered = sem("scattered")
        sums_done = sem("sums_done")
        agg_ready = sem("agg_ready")
        agg_turned = sem("agg_turned")
        y_ready = sem("y_ready")
        y_mean = sem("y_mean")
        centred = sem("centred")
        squared = sem("squared")
        y_var = sem("y_var")
        y_std = sem("y_std")
        y_rstd = sem("y_rstd")
        normed = sem("normed")
        stored = sem("stored")

        block = ctx.enter_context(nc.Block())

        def halves(t):
            for h in range(2):
                lo = h * HALF
                yield h, t[lo:lo + FULL * P, :].rearrange("(j p) c -> p j c", p=P), \
                    t[lo + FULL * P:lo + FULL * P + HTAIL[h], :]

        N_TABLES = 8 * 16

        @block.sync
        def _(sp):
            sp.wait_ge(s_pre, 1)
            for h, whole, last in halves(x):
                sp.dma_start(x_sb[:, 0:FULL, h, :], whole).then_inc(s_x, 16)
                sp.dma_start(x_sb[0:HTAIL[h], FULL, h, :], last).then_inc(s_x, 16)
            for i, v in enumerate((src, dst)):
                sp.dma_start(index[:, i, 0:EPP], v[0:P * EPP].rearrange("(p t) -> p t", t=EPP)).then_inc(s_edges, 16)
                sp.dma_start(index[0:TAIL, i, EPP:TILES], v[P * EPP:E].rearrange("(p t) -> p t", t=1)).then_inc(s_edges, 16)
            sp.dma_start(basis_sb[:, 0:EPP, :], basis[0:P * EPP, :].rearrange("(p t) b -> p t b", t=EPP)).then_inc(s_edges, 16)
            sp.dma_start(basis_sb[0:TAIL, EPP, :], basis[P * EPP:E, :]).then_inc(s_edges, 16)
            sp.wait_ge(s_abc, (BLK + 1) // 2)
            for h, whole, last in halves(a_table):
                sp.dma_start(whole, ab_sb[:, 0:FULL, 0, h, :]).then_inc(s_tables, 16)
                sp.dma_start(last, ab_sb[0:HTAIL[h], FULL, 0, h, :]).then_inc(s_tables, 16)
            for q in range(4):
                lo, hi = 4 * q, min(4 * q + 4, BLK)
                sp.wait_ge(normed, q + 1)
                for h, whole, last in halves(out):
                    if hi <= FULL:
                        sp.dma_start(whole[:, lo:hi, :], y[:, lo:hi, h, :]).then_inc(stored, 16)
                    else:
                        sp.dma_start(last, y[0:HTAIL[h], FULL, h, :]).then_inc(stored, 16)
            sp.wait_ge(stored, 16 * 8)

        @block.gpsimd
        def _(pool):
            pool.memset(ident[:, :], 0.0).then_inc(s_ident, 1)
            pool.wait_ge(s_ident, 1)
            pool.affine_select(out=ident[:, :], in_=ident[:, :], compare_op=ALU.not_equal, fill=1.0,
                               base=0, pattern=[[-1, P]], channel_multiplier=1).then_inc(s_ident, 1)
            pool.iota(node_i[:, :], pattern=[[1, HALF]], base=0, channel_multiplier=0).then_inc(s_iota, 1)

            def gather(g, slot, first):
                pool.wait_ge(staged, g + 1)
                if not first:
                    pool.wait_ge(h_added, g - 1)
                pool.sem_inc(pool_turns, 1)
                for t in range(TG):
                    for i, table in enumerate((a_table, b_table)):
                        pool.indirect_dma_start(
                            rows[:, slot, i, t, :], None, table[:, :],
                            bass.IndirectOffsetOnAxis(stage[:, slot, i, t:t + 1].bitcast(U32), 0)
                        ).then_inc(gathered[slot], 16)

            pool.wait_ge(s_tables, N_TABLES)
            gather(0, 0, True)
            gather(1, 1, True)
            with pool.Fori(1, GROUPS // 2) as i:
                gather(2 * i, 0, False)
                gather(2 * i + 1, 1, False)

        @block.vector
        def _(dve):
            v = nc.vector
            step = [0]

            def chain(inst):
                step[0] += 1
                inst.then_inc(s_dve, 1)
                dve.wait_ge(s_dve, step[0])

            v.memset(index[:, :, EPP:TILES], 0)
            v.memset(basis_sb[:, EPP, :], 0.0)
            v.memset(w_diag[:, :, :], 0.0)
            v.memset(w1_diag[:, :, :, :], 0.0)
            v.memset(b1_row[:, :, :, :], 0.0)
            v.memset(mask[:, :, :], 0.0)
            v.memset(row_f[:, :], 0.0)
            v.memset(zeros[:, :], 0.0)
            v.memset(ones3[:, :], 1.0)
            v.memset(eps[:, :], 1e-5)
            v.memset(y[:, FULL, :, :], 0.0)
            v.memset(x_sb[:, FULL, :, :], 0.0).then_inc(s_pre, 1)

            for b in range(4):
                dve.wait_ge(s_xt, b + 1)
                n = min(512, BLK * P - 512 * b)
                v.tensor_copy(x_turned[:, 512 * b:512 * b + n], bank[b][:, 0:n]).then_inc(s_xc, 1)
            dve.wait_ge(s_w, 16 * 12)
            for q in range((BLK + 1) // 2):
                dve.wait_ge(s_ab, q + 1)
                k = min(2, BLK - 2 * q)
                v.tensor_tensor(ab_sb[:, 2 * q:2 * q + k, :, :, :].rearrange("p j a h c -> p j (a h c)"),
                                bank[q][:, 0:k * 256].rearrange("p (j n) -> p j n", n=256),
                                b1_row[:, :, :, :].rearrange("p a h c -> p (a h c)").unsqueeze(1).to_broadcast([P, k, 256]),
                                ALU.add).then_inc(s_abc, 1)
            dve.wait_ge(s_w2t, 1)
            v.tensor_copy(w2_turned[:, :, :], bank[4][0:H, :].rearrange("j (b k) -> j b k", k=H)).then_inc(s_w2c, 1)
            dve.wait_ge(s_v, 1)
            v.tensor_copy(v_sb[:, :, :], bank[5][:, 0:CH * C].rearrange("p (q c) -> p q c", c=C)).then_inc(s_vc, 1)

            chain(v.tensor_copy(bias_b16[:, :], iib3[:, :]))
            chain(v.tensor_copy(bias_parts[:, 0, :], bias_b16[:, :]))
            chain(v.tensor_tensor(bias_left[:, 0, :], iib3[:, :], bias_parts[:, 0, :], ALU.subtract))
            chain(v.tensor_copy(bias_b16[:, :], bias_left[:, 0, :]))
            chain(v.tensor_copy(bias_parts[:, 1, :], bias_b16[:, :]))
            chain(v.tensor_tensor(bias_parts[:, 2, :], bias_left[:, 0, :], bias_parts[:, 1, :], ALU.subtract))
            dve.wait_ge(s_ident, 2)
            chain(v.tensor_scalar(bias_mix[:, 0, :], bias_parts[:, 0, :], ident[0:3, 0:1], None, ALU.mult))
            chain(v.scalar_tensor_tensor(out=bias_mix[:, 1, :], in0=bias_parts[:, 1, :], scalar=ident[0:3, 1:2],
                                         in1=bias_mix[:, 0, :], op0=ALU.mult, op1=ALU.add))
            chain(v.scalar_tensor_tensor(out=bias_mix[:, 0, :], in0=bias_parts[:, 2, :], scalar=ident[0:3, 2:3],
                                         in1=bias_mix[:, 1, :], op0=ALU.mult, op1=ALU.add))
            v.tensor_copy(bias3[:, :, :], bias_mix[:, 0, :].unsqueeze(1).to_broadcast([3, TG, C])).then_inc(s_bias, 1)

            dve.wait_ge(s_edges, 16 * 6)

            def stage_index(g, slot):
                v.tensor_copy(stage[:, slot, :, :], index[:, :, bass.ds(TG * g, TG)]).then_inc(staged, 1)

            stage_index(0, 0)
            stage_index(1, 1)

            dve.wait_ge(s_iota, 1)
            v.tensor_copy(node_row[:, :], node_i[:, :])
            chain(v.tensor_copy(src_f[:, :], index[:, 0, :]))
            chain(v.tensor_scalar(upper[:, :], src_f[:, :], float(HALF), None, ALU.is_ge))
            for rows_of, cols in ((slice(0, P), slice(0, EPP)), (slice(0, TAIL), slice(EPP, TILES))):
                v.scalar_tensor_tensor(out=row_f[rows_of, cols], in0=upper[rows_of, cols], scalar=-float(HALF),
                                       in1=src_f[rows_of, cols], op0=ALU.mult, op1=ALU.add)
                v.tensor_scalar(mask[rows_of, cols, 0], upper[rows_of, cols], -1.0, 1.0, ALU.mult, ALU.add)
                last = v.tensor_copy(mask[rows_of, cols, 1], upper[rows_of, cols])
            chain(last)

            def front_group(g, pair, slot, first, stage_next):
                dve.wait_ge(gathered[slot], 2 * TG * 16 * (pair + 1))
                if stage_next:
                    stage_index(g + 2, slot)
                v.tensor_tensor(h_sb[:, slot, :, :], rows[:, slot, 0, :, :], rows[:, slot, 1, :, :],
                                ALU.add).then_inc(h_added, 1)
                if not first:
                    dve.wait_ge(transposed, TG * (g - 1))
                dve.wait_ge(h_added, g + 1)
                for t in range(TG):
                    v.tensor_tensor(weighted[:, slot, t, :, :],
                                    h_sb[:, slot, t, :].unsqueeze(1).to_broadcast([P, NB, H]),
                                    basis_sb[:, bass.ds(TG * g + t, 1), :].rearrange("p o b -> p (o b)").unsqueeze(2).to_broadcast([P, NB, H]),
                                    ALU.mult).then_inc(weighed, 1)

            def back_group(g, slot, first):
                if not first:
                    dve.wait_ge(scattered, TG * (g - 1))
                for t in range(TG):
                    v.tensor_scalar(onehot[:, slot, t, :], node_row[:, :], row_f[:, bass.ds(TG * g + t, 1)], None,
                                    ALU.is_equal).then_inc(onehot_ready, 1)
                dve.wait_ge(activated, g + 1)
                v.tensor_tensor(split[:, slot, 1, :, :], msg[:, slot, :, :], split[:, slot, 0, :, :],
                                ALU.subtract).then_inc(rest_ready, 1)
                dve.wait_ge(rest_ready, g + 1)
                for part in range(2):
                    last = v.tensor_tensor(parts[:, slot, part, :, :, :],
                                           split[:, slot, part, :, :].unsqueeze(2).to_broadcast([P, TG, 2, C]),
                                           mask[:, bass.ds(TG * g, TG), :].unsqueeze(3).to_broadcast([P, TG, 2, C]),
                                           ALU.mult)
                last.then_inc(parts_ready, 1)

            front_group(0, 0, 0, True, True)
            front_group(1, 0, 1, True, True)
            back_group(0, 0, True)
            front_group(2, 1, 0, False, True)
            back_group(1, 1, True)
            front_group(3, 1, 1, False, True)
            back_group(2, 0, False)
            with dve.Fori(2, GROUPS // 2 - 1) as i:
                front_group(2 * i, i, 0, False, True)
                back_group(2 * i - 1, 1, False)
                front_group(2 * i + 1, i, 1, False, True)
                back_group(2 * i, 0, False)
            front_group(GROUPS - 2, GROUPS // 2 - 1, 0, False, False)
            back_group(GROUPS - 3, 1, False)
            front_group(GROUPS - 1, GROUPS // 2 - 1, 1, False, False)
            back_group(GROUPS - 2, 0, False)
            back_group(GROUPS - 1, 1, False)

            for b in (0, 2):
                dve.wait_ge(sums_done, 1)
                v.tensor_copy(agg[:, b * SB_COLS:(b + 1) * SB_COLS], sums_ps[b][:, 0:SB_COLS]).then_inc(agg_ready, 1)

            for q in range(4):
                dve.wait_ge(agg_turned, q + 1)
                lo, hi = 4 * q, min(4 * q + 4, BLK)
                k = hi - lo
                np_ = P if hi <= FULL else HTAIL[0]
                blocks = (slice(None), slice(lo, hi))
                v.scalar_tensor_tensor(out=y[0:np_, lo:hi, :, :].rearrange("p j h c -> p (j h c)"),
                                       in0=x_sb[0:np_, lo:hi, :, :].rearrange("p j h c -> p (j h c)"), scalar=2.0,
                                       in1=bank[4 + q][0:np_, 0:k * P], op0=ALU.mult, op1=ALU.add).then_inc(y_ready, 1)
                dve.wait_ge(y_ready, q + 1)
                v.tensor_reduce(mean[blocks], y[blocks], axis=AX.X, op=ALU.add).then_inc(y_mean, 1)
                dve.wait_ge(y_mean, 2 * q + 1)
                v.tensor_scalar(mean[blocks], mean[blocks], 1.0 / C, None, ALU.mult).then_inc(y_mean, 1)
                dve.wait_ge(y_mean, 2 * q + 2)
                v.tensor_tensor(y[blocks], y[blocks], mean[blocks].unsqueeze(3).to_broadcast([P, k, 2, C]),
                                ALU.subtract).then_inc(centred, 1)
                dve.wait_ge(centred, q + 1)
                v.tensor_tensor(sq[blocks], y[blocks], y[blocks], ALU.mult).then_inc(squared, 1)
                dve.wait_ge(squared, q + 1)
                v.tensor_reduce(var[blocks], sq[blocks], axis=AX.X, op=ALU.add).then_inc(y_var, 1)
                dve.wait_ge(y_std, q + 1)
                v.reciprocal(rstd[blocks], std[blocks]).then_inc(y_rstd, 1)
                dve.wait_ge(y_rstd, q + 1)
                v.tensor_tensor(y[blocks], y[blocks], rstd[blocks].unsqueeze(3).to_broadcast([P, k, 2, C]),
                                ALU.mult).then_inc(normed, 1)

        @block.scalar
        def _(act):
            a = nc.scalar
            act.wait_ge(s_pre, 1)
            for h in range(2):
                part = slice(64 * h, 64 * h + 64)
                act.dma_start(w_diag[part, h, :], pp_w[:, :]).then_inc(s_w, 16)
                for tab in range(2):
                    act.dma_start(w1_diag[part, tab, h, :], pi_w1[tab * C:(tab + 1) * C, :]).then_inc(s_w, 16)
                act.dma_start(ppb_col[part, :], pp_b.rearrange("(p o) -> p o", o=1)).then_inc(s_w, 16)
                act.dma_start(b1_row[:, 0, h, :], pi_b1.rearrange("(o c) -> o c", o=1).to_broadcast([P, H])).then_inc(s_w, 16)
            act.dma_start(iib3[:, :], ii_b.rearrange("(o c) -> o c", o=1).to_broadcast([3, C])).then_inc(s_w, 16)
            act.dma_start(iiw_sb[:, :], ii_w[:, :]).then_inc(s_w, 16)
            act.dma_start(w2_sb[:, :], pi_w2[:, :]).then_inc(s_w2, 16)
            act.wait_ge(s_w, 16 * 12)
            for b in range(4):
                act.wait_ge(s_p1, b + 1)
                n = min(512, BLK * P - 512 * b)
                a.activation(p1_turned[:, 512 * b:512 * b + n], bank[4 + b][:, 0:n], ACT.Tanh,
                             bias=ppb_col[:, 0:1]).then_inc(s_th, 1)
            act.wait_ge(s_abc, (BLK + 1) // 2)
            for h, whole, last in halves(b_table):
                act.dma_start(whole, ab_sb[:, 0:FULL, 1, h, :]).then_inc(s_tables, 16)
                act.dma_start(last, ab_sb[0:HTAIL[h], FULL, 1, h, :]).then_inc(s_tables, 16)

            def group(g, slot, first):
                for t in range(TG):
                    act.wait_ge(transposed, TG * g + t + 1)
                    if not first:
                        act.wait_ge(projected, TG * (g - 1) + t + 1)
                    a.activation(turned[:, t, :, :], turn_ps[t % 2][:, :].rearrange("p (q e) -> p q e", e=P),
                                 ACT.Copy).then_inc(copied, 1)
                act.wait_ge(projected, TG * (g + 1))
                if not first:
                    act.wait_ge(parts_ready, g - 1)
                z = z_ps[slot][:, 0:TG * C].rearrange("p (t c) -> p t c", c=C)
                a.activation(msg[:, slot, :, :], z, ACT.Tanh)
                a.activation(split[:, slot, 0, :, :], z, ACT.Tanh).then_inc(activated, 1)

            group(0, 0, True)
            group(1, 1, False)
            with act.Fori(1, GROUPS // 2) as i:
                group(2 * i, 0, False)
                group(2 * i + 1, 1, False)

            for b in (1, 3):
                act.wait_ge(sums_done, 1)
                a.activation(agg[:, b * SB_COLS:(b + 1) * SB_COLS], sums_ps[b][:, 0:SB_COLS], ACT.Copy).then_inc(agg_ready, 1)
            for q in range(4):
                lo, hi = 4 * q, min(4 * q + 4, BLK)
                act.wait_ge(y_var, q + 1)
                a.activation(std[:, lo:hi, :], var[:, lo:hi, :], ACT.Sqrt, bias=eps[:, 0:1], scale=1.0 / C).then_inc(y_std, 1)

        @block.tensor
        def _(pe):
            m = nc.tensor
            pe.wait_ge(s_x, 16 * 4)
            pe.wait_ge(s_ident, 2)
            for j in range(BLK):
                last = m.transpose(bank[j // 4][:, (j % 4) * P:(j % 4 + 1) * P],
                                   x_sb[:, j, :, :].rearrange("p h c -> p (h c)"), ident[:, :])
                if j % 4 == 3 or j == BLK - 1:
                    last.then_inc(s_xt, 1)
            pe.wait_ge(s_w, 16 * 12)
            for b in range(4):
                pe.wait_ge(s_xc, b + 1)
                n = min(512, BLK * P - 512 * b)
                m.matmul(bank[4 + b][:, 0:n], w_diag[:, :, :].rearrange("p h c -> p (h c)"),
                         x_turned[:, 512 * b:512 * b + n], start=True, stop=True).then_inc(s_p1, 1)
            for j in range(BLK):
                pe.wait_ge(s_th, j // 4 + 1)
                last = m.matmul(bank[j // 2][:, (j % 2) * 256:(j % 2 + 1) * 256], p1_turned[:, j * P:(j + 1) * P],
                                w1_diag[:, :, :, :].rearrange("p a h c -> p (a h c)"), start=True, stop=True)
                if j % 2 == 1 or j == BLK - 1:
                    last.then_inc(s_ab, 1)
            pe.wait_ge(s_w2, 16)
            pe.wait_ge(s_abc, (BLK + 1) // 2)
            w2_b = w2_sb[:, :].rearrange("k (j b) -> k b j", b=NB)
            for b in range(NB):
                last = m.transpose(bank[4][0:H, b * H:(b + 1) * H], w2_b[:, b, :], ident[0:H, 0:H])
            last.then_inc(s_w2t, 1)
            pe.wait_ge(s_w2c, 1)
            for q in range(CH):
                last = m.matmul(bank[5][:, q * C:(q + 1) * C],
                                w2_turned[:, 2 * q:2 * q + 2, :].rearrange("j b k -> j (b k)"), iiw_sb[:, :],
                                start=True, stop=True)
            last.then_inc(s_v, 1)
            for b in range(4):
                m.matmul(sums_ps[b][:, 0:SB_COLS], zeros[:, 0:P], zeros[:, 0:SB_COLS], start=True, stop=False,
                         skip_group_check=True)
            pe.wait_ge(s_vc, 1)
            pe.wait_ge(s_bias, 1)

            def transpose_tile(g, slot, t, first):
                pe.wait_ge(weighed, TG * g + t + 1)
                if not (first and t < 2):
                    pe.wait_ge(copied, TG * g + t - 1)
                for q in range(CH):
                    last = m.transpose(turn_ps[t % 2][:, q * P:(q + 1) * P],
                                       weighted[:, slot, t, 2 * q:2 * q + 2, :].rearrange("p b k -> p (b k)"), ident[:, :])
                last.then_inc(transposed, 1)

            def project_tile(g, slot, t, first):
                if t == 0:
                    if not first:
                        pe.wait_ge(activated, g - 1)
                    m.matmul(z_ps[slot][:, 0:TG * C], ones3[:, :], bias3[:, :, :].rearrange("p t c -> p (t c)"),
                             start=True, stop=False, skip_group_check=True)
                pe.wait_ge(copied, TG * g + t + 1)
                for q in range(CH):
                    last = m.matmul(z_ps[slot][:, t * C:(t + 1) * C], turned[:, t, q, :], v_sb[:, q, :],
                                    start=False, stop=(q == CH - 1 and t == TG - 1), skip_group_check=True)
                last.then_inc(projected, 1)

            def scatter_tile(g, slot, t):
                if t == 0:
                    pe.wait_ge(parts_ready, g + 1)
                pe.wait_ge(onehot_ready, TG * g + t + 1)
                for part in range(2):
                    for b in range(4):
                        last = m.matmul(sums_ps[b][:, 0:SB_COLS],
                                        parts[:, slot, part, t, :, :].rearrange("p h c -> p (h c)"),
                                        onehot[:, slot, t, b * SB_COLS:(b + 1) * SB_COLS],
                                        start=False, stop=False, skip_group_check=True)
                last.then_inc(scattered, 1)

            def group(g, slot, first, back):
                transpose_tile(g, slot, 0, first)
                for t in range(TG):
                    if t + 1 < TG:
                        transpose_tile(g, slot, t + 1, first)
                    if back:
                        scatter_tile(g - 2, slot, t)
                    project_tile(g, slot, t, first)

            group(0, 0, True, False)
            group(1, 1, False, False)
            with pe.Fori(1, GROUPS // 2) as i:
                group(2 * i, 0, False, True)
                group(2 * i + 1, 1, False, True)
            for t in range(TG):
                scatter_tile(GROUPS - 2, 0, t)
            for t in range(TG):
                scatter_tile(GROUPS - 1, 1, t)
            for b in range(4):
                last = m.matmul(sums_ps[b][:, 0:SB_COLS], zeros[:, 0:P], zeros[:, 0:SB_COLS], start=False, stop=True,
                                skip_group_check=True)
            last.then_inc(sums_done, 1)

            pe.wait_ge(agg_ready, 4)
            pe.wait_ge(activated, GROUPS)
            for j in range(BLK):
                n = P if j < FULL else HTAIL[0]
                last = m.transpose(bank[4 + j // 4][0:n, (j % 4) * P:(j % 4 + 1) * P], agg[:, j * P:j * P + n], ident[:, :])
                if j % 4 == 3 or j == BLK - 1:
                    last.then_inc(agg_turned, 1)


_INS = ['x', 'src', 'dst', 'edge_attr_8', 'L0_gnn_pp_W', 'L0_gnn_pp_b', 'L0_gnn_pi_W1', 'L0_gnn_pi_b1',
        'L0_gnn_pi_W2', 'L0_gnn_ii_W', 'L0_gnn_ii_b']


def kernel(**inputs):
    import numpy as _np
    import concourse.bacc as _bacc
    from concourse import mybir as _mybir
    from concourse.bass_utils import run_bass_kernel_spmd as _run

    nc = _bacc.Bacc("TRN2", target_bir_lowering=False, num_devices=1)
    arrays, args = {}, []
    for name in _INS:
        a = _np.ascontiguousarray(inputs[name])
        arrays[f"in_{name}_dram"] = a
        args.append(nc.dram_tensor(f"in_{name}_dram", a.shape, _mybir.dt.from_np(a.dtype), kind="ExternalInput").ap())
    shape = inputs['x'].shape
    args.append(nc.dram_tensor("out_0_dram", tuple(shape), _mybir.dt.float32, kind="ExternalOutput").ap())
    gnn_residual_norm_kernel(nc, *args)
    r = _run(nc, [arrays], core_ids=[0])
    return r.results[0]["out_0_dram"]
```

```python
import concourse.bass as bass
from concourse import mybir
from contextlib import ExitStack

F32 = mybir.dt.float32
F16 = mybir.dt.float16
BF16 = mybir.dt.bfloat16
I32 = mybir.dt.int32
U32 = mybir.dt.uint32
ALU = mybir.AluOpType
ACT = mybir.ActivationFunctionType
AX = mybir.AxisListType


def gnn_residual_norm_kernel(nc, x, src, dst, basis, pp_w, pp_b, pi_w1, pi_b1, pi_w2, ii_w, ii_b, out):
    P = 128
    N, C = x.shape
    E = src.shape[0]
    NB = basis.shape[1]
    H = ii_w.shape[0]
    EPP = E // P
    TAIL = E - P * EPP
    TG = 4
    TA = 3
    TILES = EPP + 1
    GROUPS = TILES // TG
    assert TILES % (2 * TG) == 0 and TAIL <= P and C == H == 64
    HALF = (N + 1) // 2 + 1
    REST = N - HALF
    SB_COLS = HALF // 4
    assert HALF % 4 == 0 and SB_COLS <= 512
    FULL = HALF // P
    BLK = FULL + 1
    HTAIL = (HALF - FULL * P, REST - FULL * P)

    a_table = nc.dram_tensor("a_table", (N, H), F32, kind="Internal").ap()
    b_table = nc.dram_tensor("b_table", (N, H), F32, kind="Internal").ap()

    ctx = ExitStack()
    with ctx:
        def sb(name, shape, dt=F32):
            return ctx.enter_context(nc.sbuf_tensor(name, shape, dt))

        def sem(name):
            return ctx.enter_context(nc.semaphore(name))

        bank = [ctx.enter_context(nc.psum_tensor(f"bank{i}", [P, 512], F32)) for i in range(8)]
        sums_ps = bank[0:4]
        hv_ps = bank[4:6]
        turn_ps = bank[6:8]

        index = sb("index", [P, 2, TILES], I32)
        basis_sb = sb("basis_sb", [P, TILES, NB])
        x_sb = sb("x_sb", [P, BLK, 2, C])
        w_diag = sb("w_diag", [P, 2, C])
        w1_diag = sb("w1_diag", [P, 2, 2, H])
        b1_row = sb("b1_row", [P, 2, 2, H])
        ppb_col = sb("ppb_col", [P, 1])
        w2_sb = sb("w2_sb", [H, H * NB])
        iiw_sb = sb("iiw_sb", [H, C])
        ident = sb("ident", [P, P])
        node_i = sb("node_i", [P, HALF], I32)
        node_row = sb("node_row", [P, HALF], F16)
        x_turned = sb("x_turned", [P, BLK * P])
        p1_turned = sb("p1_turned", [P, BLK * P])
        ab_sb = sb("ab_sb", [P, BLK, 2, 2, H])
        ident16 = sb("ident16", [P, P], F16)
        w2_turned = sb("w2_turned", [H, NB, 2, H])
        v_f = sb("v_f", [P, NB * C])
        v_parts = sb("v_parts", [P, 2, NB * C], F16)
        zeros = sb("zeros", [P, 512], BF16)
        src_f = sb("src_f", [P, TILES])
        upper = sb("upper", [P, TILES])
        place = sb("place", [P, TILES, 3])
        stage = sb("stage", [P, 2, 2, TG], I32)
        rows = sb("rows", [P, 2, 2, TG, H])
        basis_g = sb("basis_g", [P, 2, TG, NB])
        place_g = sb("place_g", [P, 2, TG, 3])
        h_sb = sb("h_sb", [P, 2, TG, H])
        h_parts = sb("h_parts", [P, 2, TG, 2, H], F16)
        h_turned = sb("h_turned", [P, 2, TG, P], F16)
        prod = sb("prod", [P, 2, TG, NB + 1, C])
        z_sb = sb("z_sb", [P, 2, TG, C])
        msg = sb("msg", [P, 2, TG, C])
        split = sb("split", [P, 2, TG, 2, C], F16)
        parts = sb("parts", [P, 2, TG, 2, 2, C], F16)
        onehot = sb("onehot", [P, 2, TG, HALF], F16)
        agg = sb("agg", [P, HALF])
        y = sb("y", [P, BLK, 2, C])
        sq = sb("sq", [P, BLK, 2, C])
        mean = sb("mean", [P, BLK, 2])
        var = sb("var", [P, BLK, 2])
        std = sb("std", [P, BLK, 2])
        rstd = sb("rstd", [P, BLK, 2])
        eps = sb("eps", [P, 1])

        s_index = sem("s_index")
        s_basis = sem("s_basis")
        s_iib = sem("s_iib")
        s_x = sem("s_x")
        s_w = sem("s_w")
        s_w2 = sem("s_w2")
        s_pre = sem("s_pre")
        s_ident = sem("s_ident")
        s_iota = sem("s_iota")
        s_dve = sem("s_dve")
        s_xt = sem("s_xt")
        s_xc = sem("s_xc")
        s_p1 = sem("s_p1")
        s_th = sem("s_th")
        s_ab = sem("s_ab")
        s_abc = sem("s_abc")
        s_w2t = sem("s_w2t")
        s_w2c = sem("s_w2c")
        s_v = sem("s_v")
        s_vc = sem("s_vc")
        s_tables = sem("s_tables")
        staged = sem("staged")
        pool_turns = sem("pool_turns")
        gathered = [sem("gathered0"), sem("gathered1")]
        h_added = sem("h_added")
        h_high = sem("h_high")
        h_ready = sem("h_ready")
        h_transposed = sem("h_transposed")
        h_copied = sem("h_copied")
        hv_ready = sem("hv_ready")
        act_products = sem("act_products")
        dve_products = sem("dve_products")
        z_ready = sem("z_ready")
        activated = sem("activated")
        placed = sem("placed")
        rest_ready = sem("rest_ready")
        parts_ready = sem("parts_ready")
        onehot_ready = sem("onehot_ready")
        scattered = sem("scattered")
        sums_done = sem("sums_done")
        agg_ready = sem("agg_ready")
        agg_turned = sem("agg_turned")
        y_ready = sem("y_ready")
        y_mean = sem("y_mean")
        centred = sem("centred")
        squared = sem("squared")
        y_var = sem("y_var")
        y_std = sem("y_std")
        y_rstd = sem("y_rstd")
        normed = sem("normed")
        stored = sem("stored")

        block = ctx.enter_context(nc.Block())

        def halves(t):
            for h in range(2):
                lo = h * HALF
                yield h, t[lo:lo + FULL * P, :].rearrange("(j p) c -> p j c", p=P), \
                    t[lo + FULL * P:lo + FULL * P + HTAIL[h], :]

        N_TABLES = 8 * 16

        @block.sync
        def _(sp):
            sp.wait_ge(s_pre, 1)
            for h, whole, last in halves(x):
                sp.dma_start(x_sb[:, 0:FULL, h, :], whole).then_inc(s_x, 16)
                sp.dma_start(x_sb[0:HTAIL[h], FULL, h, :], last).then_inc(s_x, 16)
            for i, v in enumerate((src, dst)):
                sp.dma_start(index[:, i, 0:EPP], v[0:P * EPP].rearrange("(p t) -> p t", t=EPP)).then_inc(s_index, 16)
                sp.dma_start(index[0:TAIL, i, EPP:TILES], v[P * EPP:E].rearrange("(p t) -> p t", t=1)).then_inc(s_index, 16)
            sp.wait_ge(s_abc, (BLK + 1) // 2)
            for h, whole, last in halves(a_table):
                sp.dma_start(whole, ab_sb[:, 0:FULL, 0, h, :]).then_inc(s_tables, 16)
                sp.dma_start(last, ab_sb[0:HTAIL[h], FULL, 0, h, :]).then_inc(s_tables, 16)
            sp.dma_start(basis_sb[:, 0:EPP, :], basis[0:P * EPP, :].rearrange("(p t) b -> p t b", t=EPP)).then_inc(s_basis, 16)
            sp.dma_start(basis_sb[0:TAIL, EPP, :], basis[P * EPP:E, :]).then_inc(s_basis, 16)
            for q in range(4):
                lo, hi = 4 * q, min(4 * q + 4, BLK)
                sp.wait_ge(normed, q + 1)
                for h, whole, last in halves(out):
                    if hi <= FULL:
                        sp.dma_start(whole[:, lo:hi, :], y[:, lo:hi, h, :]).then_inc(stored, 16)
                    else:
                        sp.dma_start(last, y[0:HTAIL[h], FULL, h, :]).then_inc(stored, 16)
            sp.wait_ge(stored, 16 * 8)

        @block.gpsimd
        def _(pool):
            pool.memset(ident[:, :], 0.0).then_inc(s_ident, 1)
            pool.wait_ge(s_ident, 1)
            pool.affine_select(out=ident[:, :], in_=ident[:, :], compare_op=ALU.not_equal, fill=1.0,
                               base=0, pattern=[[-1, P]], channel_multiplier=1).then_inc(s_ident, 1)
            pool.iota(node_i[:, :], pattern=[[1, HALF]], base=0, channel_multiplier=0).then_inc(s_iota, 1)

            def gather(g, slot, first):
                pool.wait_ge(staged, g + 1)
                if not first:
                    pool.wait_ge(h_added, g - 1)
                pool.sem_inc(pool_turns, 1)
                for t in range(TG):
                    for i, table in enumerate((a_table, b_table)):
                        pool.indirect_dma_start(
                            rows[:, slot, i, t, :], None, table[:, :],
                            bass.IndirectOffsetOnAxis(stage[:, slot, i, t:t + 1].bitcast(U32), 0)
                        ).then_inc(gathered[slot], 16)

            pool.wait_ge(s_tables, N_TABLES)
            gather(0, 0, True)
            gather(1, 1, True)
            with pool.Fori(1, GROUPS // 2) as i:
                gather(2 * i, 0, False)
                gather(2 * i + 1, 1, False)

        @block.vector
        def _(dve):
            v = nc.vector
            step = [0]

            def chain(inst):
                step[0] += 1
                inst.then_inc(s_dve, 1)
                dve.wait_ge(s_dve, step[0])

            v.memset(x_sb[:, FULL, :, :], 0.0)
            v.memset(w_diag[:, :, :], 0.0)
            v.memset(w1_diag[:, :, :, :], 0.0)
            v.memset(b1_row[:, :, :, :], 0.0)
            v.memset(index[:, :, EPP:TILES], 0)
            v.memset(basis_sb[:, EPP, :], 0.0).then_inc(s_pre, 1)
            v.memset(place[:, EPP:TILES, :], 0.0)
            v.memset(zeros[:, :], 0.0)
            v.memset(eps[:, :], 1e-5)
            v.memset(y[:, FULL, :, :], 0.0)
            dve.wait_ge(s_ident, 2)
            v.tensor_copy(ident16[:, :], ident[:, :])

            def stage_index(g, slot):
                v.tensor_copy(stage[:, slot, :, :], index[:, :, bass.ds(TG * g, TG)]).then_inc(staged, 1)

            dve.wait_ge(s_index, 16 * 4)
            stage_index(0, 0)
            stage_index(1, 1)

            for b in range(4):
                dve.wait_ge(s_xt, b + 1)
                n = min(512, BLK * P - 512 * b)
                v.tensor_copy(x_turned[:, 512 * b:512 * b + n], bank[b][:, 0:n]).then_inc(s_xc, 1)
            dve.wait_ge(s_w, 16 * 11)
            for q in range((BLK + 1) // 2):
                dve.wait_ge(s_ab, q + 1)
                k = min(2, BLK - 2 * q)
                v.tensor_tensor(ab_sb[:, 2 * q:2 * q + k, :, :, :].rearrange("p j a h c -> p j (a h c)"),
                                bank[q][:, 0:k * 256].rearrange("p (j n) -> p j n", n=256),
                                b1_row[:, :, :, :].rearrange("p a h c -> p (a h c)").unsqueeze(1).to_broadcast([P, k, 256]),
                                ALU.add).then_inc(s_abc, 1)
            dve.wait_ge(s_w2t, 1)
            v.tensor_copy(w2_turned[:, :, :, :],
                          bank[4][0:H, :].rearrange("j (b k) -> j b k", k=H).unsqueeze(2).to_broadcast([H, NB, 2, H])
                          ).then_inc(s_w2c, 1)
            dve.wait_ge(s_v, 1)
            chain(v.tensor_copy(v_f[:, :], bank[5][:, :]))
            chain(v.tensor_copy(v_parts[:, 0, :], v_f[:, :]))
            v.tensor_tensor(v_parts[:, 1, :], v_f[:, :], v_parts[:, 0, :], ALU.subtract).then_inc(s_vc, 1)

            dve.wait_ge(s_iota, 1)
            v.tensor_copy(node_row[:, :], node_i[:, :])
            chain(v.tensor_copy(src_f[:, :], index[:, 0, :]))
            chain(v.tensor_scalar(upper[:, :], src_f[:, :], float(HALF), None, ALU.is_ge))
            for rows_of, cols in ((slice(0, P), slice(0, EPP)), (slice(0, TAIL), slice(EPP, TILES))):
                v.scalar_tensor_tensor(out=place[rows_of, cols, 0], in0=upper[rows_of, cols], scalar=-float(HALF),
                                       in1=src_f[rows_of, cols], op0=ALU.mult, op1=ALU.add)
                v.tensor_scalar(place[rows_of, cols, 1], upper[rows_of, cols], -1.0, 1.0, ALU.mult, ALU.add)
                last = v.tensor_copy(place[rows_of, cols, 2], upper[rows_of, cols])
            chain(last)
            dve.wait_ge(s_basis, 16 * 2)
            dve.wait_ge(s_iib, 16 * 2 * TG)

            def take_h(g, pair, slot, stage_next):
                dve.wait_ge(gathered[slot], 2 * TG * 16 * (pair + 1))
                if stage_next:
                    stage_index(g + 2, slot)
                v.tensor_tensor(h_sb[:, slot, :, :], rows[:, slot, 0, :, :], rows[:, slot, 1, :, :],
                                ALU.add).then_inc(h_added, 1)
                v.tensor_copy(basis_g[:, slot, :, :], basis_sb[:, bass.ds(TG * g, TG), :])
                dve.wait_ge(h_added, g + 1)
                v.tensor_copy(h_parts[:, slot, :, 0, :], h_sb[:, slot, :, :]).then_inc(h_high, 1)
                dve.wait_ge(h_high, g + 1)
                v.tensor_tensor(h_parts[:, slot, :, 1, :], h_sb[:, slot, :, :], h_parts[:, slot, :, 0, :],
                                ALU.subtract).then_inc(h_ready, 1)

            def sum_products(g, slot):
                dve.wait_ge(hv_ready, TG * (g + 1))
                for t in range(TA, TG):
                    v.tensor_tensor(prod[:, slot, t, 0:NB, :], hv_ps[t % 2][:, :].rearrange("p (b c) -> p b c", c=C),
                                    basis_g[:, slot, t, :].unsqueeze(2).to_broadcast([P, NB, C]),
                                    ALU.mult).then_inc(dve_products, 1)
                dve.wait_ge(act_products, TA * (g + 1))
                dve.wait_ge(dve_products, g + 1)
                v.tensor_reduce(z_sb[:, slot, :, :], prod[:, slot, :, :, :].rearrange("p t b c -> p t c b"),
                                axis=AX.X, op=ALU.add).then_inc(z_ready, 1)

            def scatter_operands(g, slot, first):
                v.tensor_copy(place_g[:, slot, :, :], place[:, bass.ds(TG * g, TG), :]).then_inc(placed, 1)
                dve.wait_ge(placed, g + 1)
                if not first:
                    dve.wait_ge(scattered, TG * (g - 1))
                for t in range(TG):
                    v.tensor_scalar(onehot[:, slot, t, :], node_row[:, :], place_g[:, slot, t, 0:1], None,
                                    ALU.is_equal).then_inc(onehot_ready, 1)
                dve.wait_ge(activated, g + 1)
                v.tensor_tensor(split[:, slot, :, 1, :], msg[:, slot, :, :], split[:, slot, :, 0, :],
                                ALU.subtract).then_inc(rest_ready, 1)
                dve.wait_ge(rest_ready, g + 1)
                for t in range(TG):
                    for half in range(2):
                        last = v.tensor_scalar(parts[:, slot, t, :, half, :], split[:, slot, t, :, :],
                                               place_g[:, slot, t, 1 + half:2 + half], None, ALU.mult)
                last.then_inc(parts_ready, 1)

            take_h(0, 0, 0, True)
            take_h(1, 0, 1, True)
            sum_products(0, 0)
            for g in (2, 3):
                take_h(g, g // 2, g % 2, True)
                sum_products(g - 1, 1 - g % 2)
                scatter_operands(g - 2, g % 2, True)
            with dve.Fori(2, GROUPS // 2 - 1) as i:
                for slot in range(2):
                    take_h(2 * i + slot, i, slot, True)
                    sum_products(2 * i + slot - 1, 1 - slot)
                    scatter_operands(2 * i + slot - 2, slot, False)
            for g in (GROUPS - 2, GROUPS - 1):
                take_h(g, g // 2, g % 2, False)
                sum_products(g - 1, 1 - g % 2)
                scatter_operands(g - 2, g % 2, False)
            sum_products(GROUPS - 1, 1)
            scatter_operands(GROUPS - 2, 0, False)
            scatter_operands(GROUPS - 1, 1, False)

            for b in (0, 2):
                dve.wait_ge(sums_done, 1)
                v.tensor_copy(agg[:, b * SB_COLS:(b + 1) * SB_COLS], sums_ps[b][:, 0:SB_COLS]).then_inc(agg_ready, 1)

            for q in range(4):
                dve.wait_ge(agg_turned, q + 1)
                lo, hi = 4 * q, min(4 * q + 4, BLK)
                k = hi - lo
                np_ = P if hi <= FULL else HTAIL[0]
                blocks = (slice(None), slice(lo, hi))
                v.scalar_tensor_tensor(out=y[0:np_, lo:hi, :, :].rearrange("p j h c -> p (j h c)"),
                                       in0=x_sb[0:np_, lo:hi, :, :].rearrange("p j h c -> p (j h c)"), scalar=2.0,
                                       in1=bank[4 + q][0:np_, 0:k * P], op0=ALU.mult, op1=ALU.add).then_inc(y_ready, 1)
                dve.wait_ge(y_ready, q + 1)
                v.tensor_reduce(mean[blocks], y[blocks], axis=AX.X, op=ALU.add).then_inc(y_mean, 1)
                dve.wait_ge(y_mean, 2 * q + 1)
                v.tensor_scalar(mean[blocks], mean[blocks], 1.0 / C, None, ALU.mult).then_inc(y_mean, 1)
                dve.wait_ge(y_mean, 2 * q + 2)
                v.tensor_tensor(y[blocks], y[blocks], mean[blocks].unsqueeze(3).to_broadcast([P, k, 2, C]),
                                ALU.subtract).then_inc(centred, 1)
                dve.wait_ge(centred, q + 1)
                v.tensor_tensor(sq[blocks], y[blocks], y[blocks], ALU.mult).then_inc(squared, 1)
                dve.wait_ge(squared, q + 1)
                v.tensor_reduce(var[blocks], sq[blocks], axis=AX.X, op=ALU.add).then_inc(y_var, 1)
                dve.wait_ge(y_std, q + 1)
                v.reciprocal(rstd[blocks], std[blocks]).then_inc(y_rstd, 1)
                dve.wait_ge(y_rstd, q + 1)
                v.tensor_tensor(y[blocks], y[blocks], rstd[blocks].unsqueeze(3).to_broadcast([P, k, 2, C]),
                                ALU.mult).then_inc(normed, 1)

        @block.scalar
        def _(act):
            a = nc.scalar
            act.wait_ge(s_pre, 1)
            for h in range(2):
                part = slice(64 * h, 64 * h + 64)
                act.dma_start(w_diag[part, h, :], pp_w[:, :]).then_inc(s_w, 16)
                for tab in range(2):
                    act.dma_start(w1_diag[part, tab, h, :], pi_w1[tab * C:(tab + 1) * C, :]).then_inc(s_w, 16)
                act.dma_start(ppb_col[part, :], pp_b.rearrange("(p o) -> p o", o=1)).then_inc(s_w, 16)
                act.dma_start(b1_row[:, 0, h, :], pi_b1.rearrange("(o c) -> o c", o=1).to_broadcast([P, H])).then_inc(s_w, 16)
            act.dma_start(iiw_sb[:, :], ii_w[:, :]).then_inc(s_w, 16)
            act.dma_start(w2_sb[:, :], pi_w2[:, :]).then_inc(s_w2, 16)
            act.wait_ge(s_w, 16 * 11)
            for b in range(4):
                act.wait_ge(s_p1, b + 1)
                n = min(512, BLK * P - 512 * b)
                a.activation(p1_turned[:, 512 * b:512 * b + n], bank[4 + b][:, 0:n], ACT.Tanh,
                             bias=ppb_col[:, 0:1]).then_inc(s_th, 1)
            act.wait_ge(s_abc, (BLK + 1) // 2)
            for h, whole, last in halves(b_table):
                act.dma_start(whole, ab_sb[:, 0:FULL, 1, h, :]).then_inc(s_tables, 16)
                act.dma_start(last, ab_sb[0:HTAIL[h], FULL, 1, h, :]).then_inc(s_tables, 16)

            for slot in range(2):
                for t in range(TG):
                    act.dma_start(prod[:, slot, t, NB, :],
                                  ii_b.rearrange("(o c) -> o c", o=1).to_broadcast([P, C])).then_inc(s_iib, 16)

            def products(g, slot):
                act.wait_ge(h_transposed, g + 1)
                a.activation(h_turned[:, slot, :, :], turn_ps[slot][:, 0:TG * P // 2].bitcast(F16).rearrange("p (t e) -> p t e", e=P),
                             ACT.Copy).then_inc(h_copied, 1)
                for t in range(TA):
                    act.wait_ge(hv_ready, TG * g + t + 1)
                    for b in range(NB):
                        last = a.activation(prod[:, slot, t, b, :], hv_ps[t % 2][:, b * C:(b + 1) * C], ACT.Copy,
                                            scale=basis_g[:, slot, t, b:b + 1])
                    last.then_inc(act_products, 1)

            def messages(g, slot, first):
                act.wait_ge(z_ready, g + 1)
                if not first:
                    act.wait_ge(parts_ready, g - 1)
                a.activation(msg[:, slot, :, :], z_sb[:, slot, :, :], ACT.Tanh)
                a.activation(split[:, slot, :, 0, :], z_sb[:, slot, :, :], ACT.Tanh).then_inc(activated, 1)

            products(0, 0)
            for g in (1, 2, 3):
                products(g, g % 2)
                messages(g - 1, 1 - g % 2, g < 3)
            with act.Fori(2, GROUPS // 2) as i:
                for slot in range(2):
                    products(2 * i + slot, slot)
                    messages(2 * i + slot - 1, 1 - slot, False)
            messages(GROUPS - 1, 1, False)

            for b in (1, 3):
                act.wait_ge(sums_done, 1)
                a.activation(agg[:, b * SB_COLS:(b + 1) * SB_COLS], sums_ps[b][:, 0:SB_COLS], ACT.Copy).then_inc(agg_ready, 1)
            for q in range(4):
                lo, hi = 4 * q, min(4 * q + 4, BLK)
                act.wait_ge(y_var, q + 1)
                a.activation(std[:, lo:hi, :], var[:, lo:hi, :], ACT.Sqrt, bias=eps[:, 0:1], scale=1.0 / C).then_inc(y_std, 1)

        @block.tensor
        def _(pe):
            m = nc.tensor
            pe.wait_ge(s_x, 16 * 4)
            pe.wait_ge(s_ident, 2)
            for j in range(BLK):
                last = m.transpose(bank[j // 4][:, (j % 4) * P:(j % 4 + 1) * P],
                                   x_sb[:, j, :, :].rearrange("p h c -> p (h c)"), ident[:, :])
                if j % 4 == 3 or j == BLK - 1:
                    last.then_inc(s_xt, 1)
            pe.wait_ge(s_w, 16 * 11)
            for b in range(4):
                pe.wait_ge(s_xc, b + 1)
                n = min(512, BLK * P - 512 * b)
                m.matmul(bank[4 + b][:, 0:n], w_diag[:, :, :].rearrange("p h c -> p (h c)"),
                         x_turned[:, 512 * b:512 * b + n], start=True, stop=True).then_inc(s_p1, 1)
            for j in range(BLK):
                pe.wait_ge(s_th, j // 4 + 1)
                last = m.matmul(bank[j // 2][:, (j % 2) * 256:(j % 2 + 1) * 256], p1_turned[:, j * P:(j + 1) * P],
                                w1_diag[:, :, :, :].rearrange("p a h c -> p (a h c)"), start=True, stop=True)
                if j % 2 == 1 or j == BLK - 1:
                    last.then_inc(s_ab, 1)
            pe.wait_ge(s_w2, 16)
            pe.wait_ge(s_abc, (BLK + 1) // 2)
            w2_b = w2_sb[:, :].rearrange("k (j b) -> k b j", b=NB)
            for b in range(NB):
                last = m.transpose(bank[4][0:H, b * H:(b + 1) * H], w2_b[:, b, :], ident[0:H, 0:H])
            last.then_inc(s_w2t, 1)
            pe.wait_ge(s_w2c, 1)
            for b in range(NB):
                last = m.matmul(bank[5][:, b * C:(b + 1) * C], w2_turned[:, b, :, :].rearrange("j d k -> j (d k)"),
                                iiw_sb[:, :], start=True, stop=True)
            last.then_inc(s_v, 1)
            for b in range(4):
                m.matmul(sums_ps[b][:, 0:SB_COLS], zeros[:, 0:P], zeros[:, 0:SB_COLS], start=True, stop=False,
                         skip_group_check=True)
            pe.wait_ge(s_vc, 1)

            def transpose_h(g, slot):
                pe.wait_ge(h_ready, g + 1)
                for t in range(TG):
                    last = m.transpose(turn_ps[slot][:, t * P // 2:(t + 1) * P // 2].bitcast(F16),
                                       h_parts[:, slot, t, :, :].rearrange("p a k -> p (a k)"), ident16[:, :])
                last.then_inc(h_transposed, 1)

            def times_v(g, slot, t, first):
                if t == 0:
                    pe.wait_ge(h_copied, g + 1)
                if t >= 2:
                    pe.wait_ge(act_products, TA * g + t - 1)
                elif not first and t == 0:
                    pe.wait_ge(act_products, TA * g)
                elif not first:
                    pe.wait_ge(dve_products, g)
                for part in range(2):
                    last = m.matmul(hv_ps[t % 2][:, :], h_turned[:, slot, t, :], v_parts[:, part, :],
                                    start=(part == 0), stop=(part == 1))
                last.then_inc(hv_ready, 1)

            def scatter_tile(g, slot, t):
                if t == 0:
                    pe.wait_ge(parts_ready, g + 1)
                pe.wait_ge(onehot_ready, TG * g + t + 1)
                for part in range(2):
                    for b in range(4):
                        last = m.matmul(sums_ps[b][:, 0:SB_COLS],
                                        parts[:, slot, t, part, :, :].rearrange("p h c -> p (h c)"),
                                        onehot[:, slot, t, b * SB_COLS:(b + 1) * SB_COLS],
                                        start=False, stop=False, skip_group_check=True)
                last.then_inc(scattered, 1)

            def group(g, slot, first=False, back=True):
                transpose_h(g, slot)
                for t in range(TG):
                    if back and t != 2:
                        scatter_tile(g - 3, 1 - slot, {0: 0, 1: 1, 3: 2}[t])
                    times_v(g, slot, t, first)
                if back:
                    scatter_tile(g - 3, 1 - slot, TG - 1)

            for g in range(4):
                group(g, g % 2, first=g == 0, back=g == 3)
            with pe.Fori(2, GROUPS // 2) as i:
                for slot in range(2):
                    group(2 * i + slot, slot)
            for g in range(GROUPS - 3, GROUPS):
                for t in range(TG):
                    scatter_tile(g, g % 2, t)
            for b in range(4):
                last = m.matmul(sums_ps[b][:, 0:SB_COLS], zeros[:, 0:P], zeros[:, 0:SB_COLS], start=False, stop=True,
                                skip_group_check=True)
            last.then_inc(sums_done, 1)

            pe.wait_ge(agg_ready, 4)
            pe.wait_ge(z_ready, GROUPS)
            for j in range(BLK):
                n = P if j < FULL else HTAIL[0]
                last = m.transpose(bank[4 + j // 4][0:n, (j % 4) * P:(j % 4 + 1) * P], agg[:, j * P:j * P + n], ident[:, :])
                if j % 4 == 3 or j == BLK - 1:
                    last.then_inc(agg_turned, 1)


_INS = ['x', 'src', 'dst', 'edge_attr_8', 'L0_gnn_pp_W', 'L0_gnn_pp_b', 'L0_gnn_pi_W1', 'L0_gnn_pi_b1',
        'L0_gnn_pi_W2', 'L0_gnn_ii_W', 'L0_gnn_ii_b']


def kernel(**inputs):
    import numpy as _np
    import concourse.bacc as _bacc
    from concourse import mybir as _mybir
    from concourse.bass_utils import run_bass_kernel_spmd as _run

    nc = _bacc.Bacc("TRN2", target_bir_lowering=False, num_devices=1)
    arrays, args = {}, []
    for name in _INS:
        a = _np.ascontiguousarray(inputs[name])
        arrays[f"in_{name}_dram"] = a
        args.append(nc.dram_tensor(f"in_{name}_dram", a.shape, _mybir.dt.from_np(a.dtype), kind="ExternalInput").ap())
    shape = inputs['x'].shape
    args.append(nc.dram_tensor("out_0_dram", tuple(shape), _mybir.dt.float32, kind="ExternalOutput").ap())
    gnn_residual_norm_kernel(nc, *args)
    r = _run(nc, [arrays], core_ids=[0])
    return r.results[0]["out_0_dram"]
```

```python
import concourse.bass as bass
from concourse import mybir
from contextlib import ExitStack

F32 = mybir.dt.float32
F16 = mybir.dt.float16
BF16 = mybir.dt.bfloat16
I32 = mybir.dt.int32
U32 = mybir.dt.uint32
ALU = mybir.AluOpType
ACT = mybir.ActivationFunctionType
AX = mybir.AxisListType


def gnn_residual_norm_kernel(nc, x, src, dst, basis, pp_w, pp_b, pi_w1, pi_b1, pi_w2, ii_w, ii_b, out):
    P = 128
    N, C = x.shape
    E = src.shape[0]
    NB = basis.shape[1]
    H = ii_w.shape[0]
    TG = 4
    DVE_TILE = 1
    TA = TG - 1
    TP = 2 * TG
    EP = P * TP
    PAIRS = -(-E // EP)
    GROUPS = 2 * PAIRS
    TILES = GROUPS * TG
    LAST = E - (PAIRS - 1) * EP
    EARLY = 2
    LFULL, LREST = LAST // TP, LAST % TP
    assert PAIRS >= 4 and LFULL and LREST and C == H == 64
    HALF = (N + 1) // 2 + 1
    REST = N - HALF
    SB_COLS = HALF // 4
    assert HALF % 4 == 0 and SB_COLS <= 512
    BLK = -(-HALF // P)
    FULL = HALF // BLK
    HTAIL = (HALF - FULL * BLK, REST - FULL * BLK)
    USED = FULL + 1
    assert all(0 < n < BLK for n in HTAIL) and 96 <= FULL < P
    TABLE_CHUNKS = ((0, 8), (8, BLK))
    assert max(HTAIL) <= 8 and REST // BLK == FULL
    SPRAY = FULL // 16 * 16
    CHUNKS = [(lo, min(lo + 4, BLK)) for lo in range(0, BLK, 4)]

    b_parts_table = nc.dram_tensor("b_parts_table", (N + P, 2 * H), F16, kind="Internal").ap()
    a_table = nc.dram_tensor("a_table", (N, H), F32, kind="Internal").ap()
    b_table = nc.dram_tensor("b_table", (N + 1, H), F32, kind="Internal").ap()
    beyond_table = nc.dram_tensor("beyond_table", (PAIRS * EP,), F16, kind="Internal").ap()

    ctx = ExitStack()
    with ctx:
        def sb(name, shape, dt=F32):
            return ctx.enter_context(nc.sbuf_tensor(name, shape, dt))

        def sem(name):
            return ctx.enter_context(nc.semaphore(name))

        bank = [ctx.enter_context(nc.psum_tensor(f"bank{i}", [P, 512], F32)) for i in range(8)]
        sums_ps = bank[0:4]
        hv_ps = bank[4:6]
        turn_ps = bank[6:8]
        BASE = 256
        WIN = TG * P // 2

        index = sb("index", [P, 3, TILES], I32)
        edge_i = sb("edge_i", [P, TILES], I32)
        lane_i = sb("lane_i", [P, 1], I32)
        lane = sb("lane", [P, 1])
        basis_sb = sb("basis_sb", [P, TILES, NB])
        x_sb = sb("x_sb", [P, 2, BLK, C])
        w_diag = sb("w_diag", [P, 2, C])
        w1_diag = sb("w1_diag", [P, 2, 2, H])
        b1_row = sb("b1_row", [P, 2, H])
        ppb_col = sb("ppb_col", [P, 1])
        w2_sb = sb("w2_sb", [H, H * NB])
        iib_row = sb("iib_row", [P, C])
        iiw_sb = sb("iiw_sb", [H, C])
        ident = sb("ident", [P, P])
        node_i = sb("node_i", [P, HALF], I32)
        node_row = sb("node_row", [P, HALF], F16)
        x_pairs = sb("x_pairs", [P, BLK, 2, C])
        x_turned = sb("x_turned", [P, BLK * USED])
        p1_turned = sb("p1_turned", [P, BLK * USED])
        ab_sb = sb("ab_sb", [P, 2, 2, BLK, H])
        ident16 = sb("ident16", [P, P], F16)
        w2_turned = sb("w2_turned", [H, NB, 2, H])
        v_f = sb("v_f", [P, NB * C])
        v_parts = sb("v_parts", [P, 2, NB * C], F16)
        zeros = sb("zeros", [P, 512], BF16)
        src_f = sb("src_f", [P, TILES])
        upper = sb("upper", [P, TILES])
        valid = sb("valid", [P, TILES])
        dst_f = sb("dst_f", [P, TILES])
        base_row = sb("base_row", [1, PAIRS])
        beyond = sb("beyond", [P, TILES], F16)
        inside = sb("inside", [P, TILES])
        outside = sb("outside", [P, TILES])
        from_n = sb("from_n", [P, TILES])
        outside_n = sb("outside_n", [P, GROUPS])
        flags = sb("flags", [1, GROUPS], I32)
        ones = sb("ones", [P, P])
        b_parts = sb("b_parts", [P, 2, BLK, 2, H], F16)
        place = sb("place", [P, TILES, 3])
        stage = sb("stage", [P, 2, 2, TG], I32)
        rows = sb("rows", [P, 2, TG, H])
        win_beyond = sb("win_beyond", [P, EP], F16)
        win_hot = sb("win_hot", [P, P, TP], F16)
        win_rows = sb("win_rows", [P, 2, H], F16)
        basis_g = sb("basis_g", [P, 2, TG, NB])
        place_g = sb("place_g", [P, 2, TG, 3])
        h_sb = sb("h_sb", [P, 2, TG, H])
        h_parts = sb("h_parts", [P, 2, TG, 2, H], F16)
        h_turned = sb("h_turned", [P, 2, TG, P], F16)
        prod = sb("prod", [P, 2, TG, NB + 1, C])
        z_sb = sb("z_sb", [P, 2, TG, C])
        msg = sb("msg", [P, 2, TG, C])
        split = sb("split", [P, 2, TG, 2, C], F16)
        parts = sb("parts", [P, 2, TG, 2, 2, C], F16)
        onehot = sb("onehot", [P, 2, TG, HALF], F16)
        agg = sb("agg", [P, USED * BLK])
        y = sb("y", [P, 2, BLK, C])
        sq = sb("sq", [P, 2, BLK, C])
        x_sum = sb("x_sum", [P, 2, BLK])
        xc = sb("xc", [P, 2, BLK, C])
        centre = sb("centre", [P, P])
        mean_of = sb("mean_of", [P, P])
        var = sb("var", [P, 2, BLK])
        std = sb("std", [P, 2, BLK])
        rstd = sb("rstd", [P, 2, BLK])
        eps = sb("eps", [P, 1])
        root_eps = sb("root_eps", [P, 1])

        s_dst = sem("s_dst")
        s_src = sem("s_src")
        s_first_basis = sem("s_first_basis")
        s_basis = sem("s_basis")
        s_iib = sem("s_iib")
        s_x = sem("s_x")
        s_w = sem("s_w")
        s_ppb = sem("s_ppb")
        s_w1 = sem("s_w1")
        s_w2 = sem("s_w2")
        s_pre = sem("s_pre")
        s_wclear = sem("s_wclear")
        s_ident = sem("s_ident")
        s_iota = sem("s_iota")
        s_dve = sem("s_dve")
        s_pairs = sem("s_pairs")
        s_xt = sem("s_xt")
        s_xc = sem("s_xc")
        s_p1 = sem("s_p1")
        s_th = sem("s_th")
        s_a_ps = sem("s_a_ps")
        s_b_ps = sem("s_b_ps")
        s_a = sem("s_a")
        s_b_high = sem("s_b_high")
        s_b = sem("s_b")
        s_w2t = sem("s_w2t")
        s_w2c = sem("s_w2c")
        s_v = sem("s_v")
        s_v_out = sem("s_v_out")
        s_vc = sem("s_vc")
        s_a_table = sem("s_a_table")
        s_b_table = sem("s_b_table")
        s_b_parts = sem("s_b_parts")
        s_b_parts_table = sem("s_b_parts_table")
        s_zeros = sem("s_zeros")
        s_edge_i = sem("s_edge_i")
        s_base = sem("s_base")
        s_base_ps = sem("s_base_ps")
        s_eps = sem("s_eps")
        s_beyond = sem("s_beyond")
        s_first_beyond = sem("s_first_beyond")
        s_beyond_table = sem("s_beyond_table")
        s_outside = sem("s_outside")
        s_flags = sem("s_flags")
        extra = sem("extra")
        rows_whole = sem("rows_whole")
        win_beyond_loaded = sem("win_beyond_loaded")
        win_rows_loaded = sem("win_rows_loaded")
        win_hot_ready = sem("win_hot_ready")
        windowed = sem("windowed")
        staged = sem("staged")
        pool_turns = sem("pool_turns")
        gathered = [sem("gathered0"), sem("gathered1")]
        h_added = sem("h_added")
        h_high = sem("h_high")
        h_ready = sem("h_ready")
        h_transposed = sem("h_transposed")
        h_copied = sem("h_copied")
        hv_ready = sem("hv_ready")
        act_products = sem("act_products")
        dve_products = sem("dve_products")
        z_ready = sem("z_ready")
        activated = sem("activated")
        placed = sem("placed")
        rest_ready = sem("rest_ready")
        parts_ready = sem("parts_ready")
        onehot_ready = sem("onehot_ready")
        scattered = sem("scattered")
        sums_done = sem("sums_done")
        agg_ready = sem("agg_ready")
        agg_turned = sem("agg_turned")
        y_ready = sem("y_ready")
        s_centre = sem("s_centre")
        squared = sem("squared")
        y_var = sem("y_var")
        y_std = sem("y_std")
        y_rstd = sem("y_rstd")
        normed = sem("normed")
        stored = sem("stored")

        block = ctx.enter_context(nc.Block())

        def by_partition(t):
            return [t[h * HALF:h * HALF + FULL * BLK, :].rearrange("(p j) c -> p j c", j=BLK) for h in range(2)]

        def last_nodes(t, h):
            lo = h * HALF + FULL * BLK
            return t[lo:lo + HTAIL[h], :].rearrange("(o j) c -> o j c", o=1)

        first_x = x[0:USED * BLK, :].rearrange("(p j) c -> p j c", j=BLK)
        second_x = by_partition(x)[1]

        def write_table(eng, table, rows_of, h, ready, done):
            for lo, hi in TABLE_CHUNKS:
                eng.wait_ge(ready, (hi + 3) // 4)
                eng.dma_start(by_partition(table)[h][:, lo:hi, :], rows_of[0:FULL, h, lo:hi, :]).then_inc(done, 16)
                if lo == 0:
                    eng.dma_start(last_nodes(table, h), rows_of[FULL:USED, h, 0:HTAIL[h], :]).then_inc(done, 16)

        N_TABLE = 16 * 2 * (len(TABLE_CHUNKS) + 1)
        b_parts_rows = b_parts[:, :, :, :, :].rearrange("p h j a k -> p h j (a k)")

        @block.sync
        def _(sp):
            sp.dma_start(x_sb[0:SPRAY, 0, :, :], first_x[0:SPRAY, :, :]).then_inc(s_x, 16)
            sp.dma_start(x_sb[0:SPRAY, 1, :, :], second_x[0:SPRAY, :, :]).then_inc(s_x, 16)
            sp.dma_start(x_sb[SPRAY:USED, 0, :, :], first_x[SPRAY:USED, :, :]).then_inc(s_x, 16)
            sp.wait_ge(s_pre, 1)
            whole = (PAIRS - 1) * EP
            for i, v, done in ((2, dst, s_dst), (0, src, s_src)):
                sp.dma_start(index[:, i, 0:TILES - TP].rearrange("p (q t) -> p q t", t=TP),
                             v[0:whole].rearrange("(q p t) -> p q t", p=P, t=TP)).then_inc(done, 16)
                sp.dma_start(index[0:LFULL, i, TILES - TP:TILES],
                             v[whole:E - LREST].rearrange("(p t) -> p t", t=TP)).then_inc(done, 16)
                sp.dma_start(index[LFULL:LFULL + 1, i, TILES - TP:TILES - TP + LREST],
                             v[E - LREST:E].rearrange("(p t) -> p t", p=1)).then_inc(done, 16)

            by_pair = basis_sb[:, :, :].rearrange("p (q t) b -> p q (t b)", t=TP)
            basis_by_pair = basis[0:whole, :].rearrange("(q p t) b -> p q (t b)", p=P, t=TP)
            sp.dma_start(by_pair[:, 0:EARLY, :], basis_by_pair[:, 0:EARLY, :]).then_inc(s_first_basis, 16)

            def load_beyond(i):
                sp.dma_start(win_beyond[:, :], beyond_table[bass.ds(i * EP, EP)].rearrange("(o e) -> o e", o=1).to_broadcast([P, EP])
                             ).then_inc(win_beyond_loaded, 16)

            def load_rows(i):
                first = sp.value_load(index[0:1, 2, bass.ds(TP * i, 1)], min_val=0, max_val=N - 1)
                sp.dma_start(win_rows[:, :, :].rearrange("p a k -> p (a k)"), b_parts_table[bass.ds(first, P), :]
                             ).then_inc(win_rows_loaded, 16)

            sp.wait_ge(s_zeros, 1)
            sp.dma_start(b_parts_table[N:N + P, :], zeros[:, 0:2 * H].bitcast(F16)).then_inc(s_b_parts_table, 16)
            sp.dma_start(b_table[N:N + 1, :], zeros[0:1, 0:2 * H].bitcast(F32)).then_inc(s_b_table, 16)
            sp.wait_ge(s_beyond, 1)
            table = beyond_table.rearrange("(q p t) -> p q t", p=P, t=TP)
            beyond_by_pair = beyond[:, :].rearrange("p (q t) -> p q t", t=TP)
            sp.dma_start(table[:, 0:EARLY, :], beyond_by_pair[:, 0:EARLY, :]).then_inc(s_first_beyond, 16)
            sp.dma_start(table[:, EARLY:PAIRS, :], beyond_by_pair[:, EARLY:PAIRS, :]).then_inc(s_beyond_table, 16)
            write_table(sp, a_table, ab_sb[:, 0], 0, s_a, s_a_table)
            sp.wait_ge(s_first_beyond, 16)
            load_beyond(0)
            for h in range(2):
                write_table(sp, b_parts_table, b_parts_rows, h, s_b_parts, s_b_parts_table)
            sp.wait_ge(s_dst, 16 * 3)
            sp.wait_ge(s_b_parts_table, N_TABLE + 16)
            load_rows(0)
            write_table(sp, b_table, ab_sb[:, 1], 0, s_b, s_b_table)

            sp.wait_ge(win_hot_ready, 1)
            load_beyond(1)
            cuts = [EARLY + (PAIRS - 1 - EARLY) * n // 3 for n in range(4)]
            for n, (lo, hi) in enumerate(zip(cuts, cuts[1:])):
                if n:
                    sp.wait_ge(windowed, n)
                sp.dma_start(by_pair[:, lo:hi, :], basis_by_pair[:, lo:hi, :]).then_inc(s_basis, 16)
                if n == 2:
                    load_rows(1)
            sp.dma_start(basis_sb[0:LFULL, TILES - TP:TILES, :],
                         basis[whole:E - LREST, :].rearrange("(p t) b -> p t b", t=TP)).then_inc(s_basis, 16)
            sp.dma_start(basis_sb[LFULL:LFULL + 1, TILES - TP:TILES - TP + LREST, :],
                         basis[E - LREST:E, :].rearrange("(p t) b -> p t b", p=1)).then_inc(s_basis, 16)
            sp.wait_ge(s_beyond_table, 16)
            with sp.Fori(2, PAIRS) as i:
                sp.wait_ge(win_hot_ready, i)
                load_beyond(i)
                sp.wait_ge(windowed, 2 * i)
                load_rows(i)
            for q, (lo, hi) in enumerate(CHUNKS):
                sp.wait_ge(normed, q + 1)
                for h, rows_out in enumerate(by_partition(out)):
                    sp.dma_start(rows_out[:, lo:hi, :], y[0:FULL, h, lo:hi, :]).then_inc(stored, 16)
                    if lo == 0:
                        sp.dma_start(last_nodes(out, h), y[FULL:USED, h, 0:HTAIL[h], :]).then_inc(stored, 16)
            sp.wait_ge(stored, 16 * (2 * len(CHUNKS) + 2))
            sp.wait_ge(s_b_table, N_TABLE + 16)

        @block.gpsimd
        def _(pool):
            pool.memset(w_diag[:, :, :], 0.0)
            pool.memset(w1_diag[:, :, :, :], 0.0).then_inc(s_wclear, 1)
            pool.memset(ident[:, :], 0.0).then_inc(s_ident, 1)
            pool.wait_ge(s_ident, 1)
            pool.affine_select(out=ident[:, :], in_=ident[:, :], compare_op=ALU.not_equal, fill=1.0,
                               base=0, pattern=[[-1, P]], channel_multiplier=1).then_inc(s_ident, 1)
            pool.iota(edge_i[:, :].rearrange("p (q t) -> p q t", t=TP), pattern=[[EP, PAIRS], [1, TP]], base=0,
                      channel_multiplier=TP).then_inc(s_edge_i, 1)
            pool.iota(lane_i[:, :], pattern=[[0, 1]], base=0, channel_multiplier=1).then_inc(s_edge_i, 1)
            pool.iota(node_i[:, :], pattern=[[1, HALF]], base=0, channel_multiplier=0).then_inc(s_iota, 1)

            def fetch(slot, i, done, **how):
                for t in range(TG):
                    pool.indirect_dma_start(
                        rows[:, slot, t, :], None, (a_table, b_table)[i][:, :],
                        bass.IndirectOffsetOnAxis(stage[:, slot, i, t:t + 1].bitcast(U32), 0), **how
                    ).then_inc(done, 16)

            def gather(g, pair, slot, first):
                pool.wait_ge(staged, g + 1)
                if not first:
                    pool.wait_ge(h_added, g - 1)
                pool.sem_inc(pool_turns, 1)
                fetch(slot, 0, gathered[slot])
                outside_here = pool.value_load(flags[0:1, bass.ds(g, 1)], min_val=0, max_val=P * TG)
                with pool.If(outside_here > 0):
                    pool.wait_ge(gathered[slot], TG * 16 * (pair + 1))
                    pool.wait_ge(s_b_table, N_TABLE + 16)
                    pool.sem_inc(pool_turns, 1)
                    fetch(slot, 1, extra, compute_op=ALU.add)
                    pool.reg_add(extra_due, extra_due, TG * 16)
                    pool.wait_ge(extra, extra_due)
                pool.sem_inc(rows_whole, 1)

            def message_parts(g, slot, first=False):
                pool.wait_ge(activated, g + 1)
                pool.wait_ge(placed, g + 1)
                pool.tensor_tensor(split[:, slot, :, 1, :], msg[:, slot, :, :], split[:, slot, :, 0, :],
                                   ALU.subtract).then_inc(rest_ready, 1)
                pool.wait_ge(rest_ready, g + 1)
                if not first:
                    pool.wait_ge(scattered, TG * (g - 1))
                for part in range(2):
                    last = pool.tensor_tensor(parts[:, slot, :, part, :, :],
                                              split[:, slot, :, part, :].unsqueeze(2).to_broadcast([P, TG, 2, C]),
                                              place_g[:, slot, :, 1:3].unsqueeze(3).to_broadcast([P, TG, 2, C]),
                                              ALU.mult)
                last.then_inc(parts_ready, 1)

            extra_due = pool.alloc_register("extra_due")
            pool.reg_mov(extra_due, 0)
            pool.wait_ge(s_flags, 1)
            pool.wait_ge(s_a_table, N_TABLE)
            gather(0, 0, 0, True)
            gather(1, 0, 1, True)
            gather(2, 1, 0, False)
            gather(3, 1, 1, False)
            message_parts(0, 0, first=True)
            gather(4, 2, 0, False)
            message_parts(1, 1, first=True)
            gather(5, 2, 1, False)
            message_parts(2, 0)
            with pool.Fori(3, PAIRS) as i:
                for slot in range(2):
                    gather(2 * i + slot, i, slot, False)
                    message_parts(2 * i + slot - 3, 1 - slot)
            for g in range(GROUPS - 3, GROUPS):
                message_parts(g, g % 2)

        @block.vector
        def _(dve):
            v = nc.vector
            step = [0]

            def chain(inst):
                step[0] += 1
                inst.then_inc(s_dve, 1)
                dve.wait_ge(s_dve, step[0])

            v.memset(eps[:, :], 1e-5).then_inc(s_eps, 1)
            v.memset(index[:, :, TILES - TP:TILES], 0)
            v.memset(basis_sb[:, TILES - TP:TILES, :], 0.0).then_inc(s_pre, 1)
            v.memset(zeros[:, :], 0.0).then_inc(s_zeros, 1)
            v.memset(ones[:, :], 1.0)
            v.memset(agg[:, HALF:USED * BLK], 0.0)
            dve.wait_ge(s_x, 16 * 6)
            for lo, hi in CHUNKS:
                v.tensor_copy(x_pairs[0:USED, lo:hi, :, :].rearrange("p j h c -> p h j c"), x_sb[0:USED, :, lo:hi, :]).then_inc(s_pairs, 1)
            dve.wait_ge(s_ident, 2)
            v.tensor_copy(ident16[:, :], ident[:, :])

            for b, (lo, hi) in enumerate(CHUNKS):
                dve.wait_ge(s_xt, b + 1)
                v.tensor_copy(x_turned[:, lo * USED:hi * USED], bank[b][:, 0:(hi - lo) * USED]).then_inc(s_xc, 1)
            dve.wait_ge(s_dst, 16 * 3)
            v.tensor_copy(base_row[:, :], index[0:1, 2, 0:TILES:TP]).then_inc(s_base, 1)
            chain(v.tensor_copy(dst_f[:, :], index[:, 2, :]))

            dve.wait_ge(s_edge_i, 2)
            v.tensor_scalar(valid[:, :], edge_i[:, :], float(E), None, ALU.is_lt)
            dve.wait_ge(s_base_ps, 1)
            v.tensor_tensor(beyond[:, :].rearrange("p (q t) -> p q t", t=TP),
                                  dst_f[:, :].rearrange("p (q t) -> p q t", t=TP),
                                  bank[3][:, BASE:BASE + PAIRS].unsqueeze(2).to_broadcast([P, PAIRS, TP]), ALU.subtract
                                  ).then_inc(s_beyond, 1)
            v.tensor_copy(lane[:, :], lane_i[:, :])
            dve.wait_ge(s_beyond, 1)
            chain(v.tensor_scalar(inside[:, :], beyond[:, :], 0.0, None, ALU.is_ge))
            chain(v.scalar_tensor_tensor(out=inside[:, :], in0=beyond[:, :], scalar=float(P), in1=inside[:, :],
                                         op0=ALU.is_lt, op1=ALU.mult))
            v.tensor_scalar(from_n[:, :], dst_f[:, :], -1.0, float(N), ALU.mult, ALU.add)
            chain(v.tensor_scalar(outside[:, :], inside[:, :], -1.0, 1.0, ALU.mult, ALU.add))
            chain(v.tensor_tensor(outside[:, :], outside[:, :], valid[:, :], ALU.mult))
            v.tensor_reduce(outside_n[:, :], outside[:, :].rearrange("p (g t) -> p g t", t=TG), axis=AX.X,
                            op=ALU.add).then_inc(s_outside, 1)
            chain(v.tensor_tensor(from_n[:, :], from_n[:, :], inside[:, :], ALU.mult))
            chain(v.tensor_tensor(index[:, 1, :], from_n[:, :], dst_f[:, :], ALU.add))

            dve.wait_ge(s_src, 16 * 3)
            def stage_index(g, slot):
                v.tensor_copy(stage[:, slot, :, :], index[:, 0:2, bass.ds(TG * g, TG)]).then_inc(staged, 1)

            stage_index(0, 0)
            stage_index(1, 1)

            def window_one_hot(i, first):
                dve.wait_ge(win_beyond_loaded, 16 * (i + 1))
                if not first:
                    dve.wait_ge(windowed, 2 * i)
                v.tensor_scalar(win_hot[:, :, :].rearrange("n p t -> n (p t)"), win_beyond[:, :], lane[:, 0:1], None,
                                ALU.is_equal).then_inc(win_hot_ready, 1)

            dve.wait_ge(s_w1, 16 * 3)
            for q, (lo, hi) in enumerate(CHUNKS):
                dve.wait_ge(s_a_ps, q + 1)
                v.tensor_tensor(ab_sb[0:USED, 0, :, lo:hi, :],
                                bank[q][0:USED, 0:(hi - lo) * P].rearrange("p (j h c) -> p h j c", h=2, c=H),
                                b1_row[0:USED, :, :].unsqueeze(2).to_broadcast([USED, 2, hi - lo, H]), ALU.add).then_inc(s_a, 1)
            v.tensor_copy(flags[:, :], bank[3][0:1, BASE:BASE + GROUPS]).then_inc(s_flags, 1)
            dve.wait_ge(s_w2t, 1)
            v.tensor_copy(w2_turned[:, :, :, :],
                          bank[0][0:H, :].rearrange("j (b k) -> j b k", k=H).unsqueeze(2).to_broadcast([H, NB, 2, H])
                          ).then_inc(s_w2c, 1)
            for q, (lo, hi) in enumerate(CHUNKS):
                dve.wait_ge(s_b_high, q + 1)
                v.tensor_tensor(b_parts[0:USED, :, lo:hi, 1, :],
                                bank[4 + q][0:USED, 0:(hi - lo) * P].rearrange("p (j h c) -> p h j c", h=2, c=H),
                                b_parts[0:USED, :, lo:hi, 0, :], ALU.subtract).then_inc(s_b_parts, 1)
            window_one_hot(0, True)
            dve.wait_ge(s_v, 1)
            v.tensor_copy(v_f[:, :], bank[1][:, :]).then_inc(s_v_out, 1)
            dve.wait_ge(s_v_out, 1)
            chain(v.tensor_copy(v_parts[:, 0, :], v_f[:, :]))
            v.tensor_tensor(v_parts[:, 1, :], v_f[:, :], v_parts[:, 0, :], ALU.subtract).then_inc(s_vc, 1)

            def take_h(g, pair, slot, stage_next):
                dve.wait_ge(gathered[slot], TG * 16 * (pair + 1))
                dve.wait_ge(rows_whole, g + 1)
                if stage_next:
                    stage_index(g + 2, slot)
                dve.wait_ge(windowed, g + 1)
                v.tensor_tensor(h_sb[:, slot, :, :], rows[:, slot, :, :],
                                turn_ps[slot][:, WIN:WIN + TG * H].rearrange("p (t k) -> p t k", k=H),
                                ALU.add).then_inc(h_added, 1)
                v.tensor_copy(basis_g[:, slot, :, :], basis_sb[:, bass.ds(TG * g, TG), :])
                dve.wait_ge(h_added, g + 1)
                v.tensor_copy(h_parts[:, slot, :, 0, :], h_sb[:, slot, :, :]).then_inc(h_high, 1)
                dve.wait_ge(h_high, g + 1)
                v.tensor_tensor(h_parts[:, slot, :, 1, :], h_sb[:, slot, :, :], h_parts[:, slot, :, 0, :],
                                ALU.subtract).then_inc(h_ready, 1)

            def products(g, slot, t=DVE_TILE):
                dve.wait_ge(hv_ready, TG * g + t + 1)
                v.tensor_tensor(prod[:, slot, t, 0:NB, :], hv_ps[t % 2][:, :].rearrange("p (b c) -> p b c", c=C),
                                basis_g[:, slot, t, :].unsqueeze(2).to_broadcast([P, NB, C]),
                                ALU.mult).then_inc(dve_products, 1)

            def sum_products(g, slot, taken=0):
                dve.wait_ge(act_products, TA * (g + 1) - taken)
                dve.wait_ge(dve_products, g + 1 + taken)
                v.tensor_reduce(z_sb[:, slot, :, :], prod[:, slot, :, :, :].rearrange("p t b c -> p t c b"),
                                axis=AX.X, op=ALU.add).then_inc(z_ready, 1)

            def one_hots(g, slot, first):
                if not first:
                    dve.wait_ge(parts_ready, g - 1)
                v.tensor_copy(place_g[:, slot, :, :], place[:, bass.ds(TG * g, TG), :]).then_inc(placed, 1)
                dve.wait_ge(placed, g + 1)
                if not first:
                    dve.wait_ge(scattered, TG * (g - 1))
                for t in range(TG):
                    v.tensor_scalar(onehot[:, slot, t, :], node_row[:, :], place_g[:, slot, t, 0:1], None,
                                    ALU.is_equal).then_inc(onehot_ready, 1)

            def group(g, pair, slot, first, more=True):
                take_h(g, pair, slot, more)
                if slot == 1 and more:
                    window_one_hot(pair + 1, False)
                sum_products(g - 1, 1 - slot)
                products(g, slot)
                one_hots(g - 1, 1 - slot, first)

            dve.wait_ge(s_first_basis, 16)
            take_h(0, 0, 0, True)
            dve.wait_ge(s_iota, 1)
            v.tensor_copy(node_row[:, :], node_i[:, :])
            chain(v.tensor_copy(src_f[:, :], index[:, 0, :]))
            chain(v.tensor_scalar(upper[:, :], src_f[:, :], float(HALF), None, ALU.is_ge))
            v.scalar_tensor_tensor(out=place[:, :, 0], in0=upper[:, :], scalar=-float(HALF), in1=src_f[:, :],
                                   op0=ALU.mult, op1=ALU.add)
            chain(v.tensor_tensor(place[:, :, 2], upper[:, :], valid[:, :], ALU.mult))
            chain(v.tensor_tensor(place[:, :, 1], valid[:, :], place[:, :, 2], ALU.subtract))

            dve.wait_ge(s_iib, 16)
            chain(v.tensor_copy(prod[:, :, :, NB, :].rearrange("p s t c -> p (s t) c"),
                                iib_row[:, :].unsqueeze(1).to_broadcast([P, 2 * TG, C])))

            products(0, 0)
            for g in (1, 2, 3):
                group(g, g // 2, g % 2, g < 3)
            dve.wait_ge(s_basis, 16 * 5)
            with dve.Fori(2, PAIRS - 1) as i:
                for slot in range(2):
                    group(2 * i + slot, i, slot, False)
            for g in (GROUPS - 2, GROUPS - 1):
                group(g, PAIRS - 1, g % 2, False, more=False)
            products(GROUPS - 1, 1, TG - 1)
            sum_products(GROUPS - 1, 1, taken=1)
            one_hots(GROUPS - 1, 1, False)

            chain(v.memset(mean_of[:, :], 0.0))
            for h in range(2):
                last = v.memset(mean_of[64 * h:64 * h + 64, C * h:C * h + C], 1.0 / C)
            chain(last)
            v.tensor_tensor(centre[:, :], ident[:, :], mean_of[:, :], ALU.subtract).then_inc(s_centre, 1)
            chain(v.tensor_reduce(x_sum[0:USED, :, :], x_sb[0:USED, :, :, :], axis=AX.X, op=ALU.add))
            chain(v.scalar_tensor_tensor(out=xc[0:USED, :, :, :].rearrange("p h j c -> p (h j) c"),
                                         in0=x_sum[0:USED, :, :].rearrange("p h j -> p (h j)").unsqueeze(2).to_broadcast([USED, 2 * BLK, C]),
                                         scalar=-1.0 / C, in1=x_sb[0:USED, :, :, :].rearrange("p h j c -> p (h j) c"),
                                         op0=ALU.mult, op1=ALU.add))
            chain(v.tensor_scalar(xc[0:USED, :, :, :], xc[0:USED, :, :, :], 2.0, None, ALU.mult))
            for b in (0, 2):
                dve.wait_ge(sums_done, b + 1)
                v.tensor_copy(agg[:, b * SB_COLS:(b + 1) * SB_COLS], sums_ps[b][:, 0:SB_COLS]).then_inc(agg_ready, 1)

            def residual(q, lo, hi):
                dve.wait_ge(agg_turned, q + 1)
                v.tensor_tensor(y[0:USED, :, lo:hi, :], xc[0:USED, :, lo:hi, :],
                                bank[4 + q][0:USED, 0:(hi - lo) * P].rearrange("p (j h c) -> p h j c", h=2, c=C),
                                ALU.add).then_inc(y_ready, 1)

            def variance(q, lo, hi):
                dve.wait_ge(squared, q + 1)
                v.tensor_reduce(var[0:USED, :, lo:hi], sq[0:USED, :, lo:hi, :], axis=AX.X, op=ALU.add).then_inc(y_var, 1)

            def normalize(q, lo, hi):
                dve.wait_ge(y_std, q + 1)
                v.reciprocal(rstd[0:USED, :, lo:hi], std[0:USED, :, lo:hi]).then_inc(y_rstd, 1)
                dve.wait_ge(y_rstd, q + 1)
                v.tensor_tensor(y[0:USED, :, lo:hi, :], y[0:USED, :, lo:hi, :],
                                rstd[0:USED, :, lo:hi].unsqueeze(3).to_broadcast([USED, 2, hi - lo, C]),
                                ALU.mult).then_inc(normed, 1)

            for q in range(len(CHUNKS) + 2):
                for stage_of, n in ((residual, q), (variance, q - 1), (normalize, q - 2)):
                    if 0 <= n < len(CHUNKS):
                        stage_of(n, *CHUNKS[n])

        @block.scalar
        def _(act):
            a = nc.scalar
            act.dma_start(x_sb[SPRAY:FULL, 1, :, :], second_x[SPRAY:FULL, :, :]).then_inc(s_x, 16)
            act.dma_start(x_sb[FULL:USED, 1, 0:HTAIL[1], :], last_nodes(x, 1)).then_inc(s_x, 16)
            act.dma_start(x_sb[FULL:USED, 1, HTAIL[1]:BLK, :], x[0:BLK - HTAIL[1], :].rearrange("(o j) c -> o j c", o=1)).then_inc(s_x, 16)
            act.wait_ge(s_wclear, 1)
            for h in range(2):
                part = slice(64 * h, 64 * h + 64)
                act.dma_start(w_diag[part, h, :], pp_w[:, :]).then_inc(s_w, 16)
            act.wait_ge(s_eps, 1)
            a.activation(root_eps[:, :], eps[:, :], ACT.Tanh)
            for h in range(2):
                act.dma_start(ppb_col[64 * h:64 * h + 64, :], pp_b.rearrange("(p o) -> p o", o=1)).then_inc(s_ppb, 16)
            for h in range(2):
                act.dma_start(w1_diag[64 * h:64 * h + 64, :, h, :], pi_w1.rearrange("(a k) c -> k a c", a=2)).then_inc(s_w1, 16)
            act.dma_start(b1_row[:, :, :], pi_b1.rearrange("(o h c) -> o h c", o=1, h=1).to_broadcast([P, 2, H])).then_inc(s_w1, 16)
            act.wait_ge(s_ppb, 16 * 2)
            for b, (lo, hi) in enumerate(CHUNKS):
                act.wait_ge(s_p1, b + 1)
                a.activation(p1_turned[:, lo * USED:hi * USED], bank[4 + b][:, 0:(hi - lo) * USED], ACT.Tanh,
                             bias=ppb_col[:, 0:1]).then_inc(s_th, 1)
            act.dma_start(iiw_sb[:, :], ii_w[:, :]).then_inc(s_w2, 16)
            act.dma_start(w2_sb[:, :], pi_w2[:, :]).then_inc(s_w2, 16)
            for q, (lo, hi) in enumerate(CHUNKS):
                act.wait_ge(s_b_ps, q + 1)
                b_ps = bank[4 + q][0:USED, 0:(hi - lo) * P].rearrange("p (j h c) -> p h j c", h=2, c=H)
                a.activation(b_parts[0:USED, :, lo:hi, 0, :], b_ps, ACT.Copy).then_inc(s_b_high, 1)
            write_table(act, a_table, ab_sb[:, 0], 1, s_a, s_a_table)
            for q, (lo, hi) in enumerate(CHUNKS):
                b_ps = bank[4 + q][0:USED, 0:(hi - lo) * P].rearrange("p (j h c) -> p h j c", h=2, c=H)
                act.wait_ge(s_b_parts, q + 1)
                a.activation(ab_sb[0:USED, 1, :, lo:hi, :], b_ps, ACT.Copy).then_inc(s_b, 1)
            write_table(act, b_table, ab_sb[:, 1], 1, s_b, s_b_table)
            act.dma_start(iib_row[:, :], ii_b.rearrange("(o c) -> o c", o=1).to_broadcast([P, C])).then_inc(s_iib, 16)

            def copy_h(g, slot):
                act.wait_ge(h_transposed, g + 1)
                a.activation(h_turned[:, slot, :, :], turn_ps[slot][:, 0:TG * P // 2].bitcast(F16).rearrange("p (t e) -> p t e", e=P),
                             ACT.Copy).then_inc(h_copied, 1)

            def products(g, slot, t):
                act.wait_ge(hv_ready, TG * g + t + 1)
                for b in range(NB):
                    last = a.activation(prod[:, slot, t, b, :], hv_ps[t % 2][:, b * C:(b + 1) * C], ACT.Copy,
                                        scale=basis_g[:, slot, t, b:b + 1])
                last.then_inc(act_products, 1)

            def messages(g, slot, first):
                act.wait_ge(z_ready, g + 1)
                if not first:
                    act.wait_ge(parts_ready, g - 1)
                a.activation(msg[:, slot, :, :], z_sb[:, slot, :, :], ACT.Tanh)
                a.activation(split[:, slot, :, 0, :], z_sb[:, slot, :, :], ACT.Tanh).then_inc(activated, 1)

            def group(g, slot, first_messages, back=True, tiles=TG):
                copy_h(g, slot)
                for t in range(tiles):
                    if t != DVE_TILE:
                        products(g, slot, t)
                    if t == 0 and back:
                        messages(g - 1, 1 - slot, first_messages)

            group(0, 0, True, back=False)
            for g in (1, 2, 3):
                group(g, g % 2, g < 3)
            with act.Fori(2, PAIRS - 1) as i:
                for slot in range(2):
                    group(2 * i + slot, slot, False)
            group(GROUPS - 2, 0, False)
            group(GROUPS - 1, 1, False, tiles=TG - 1)
            messages(GROUPS - 1, 1, False)

            a.activation(root_eps[:, :], eps[:, :], ACT.Sqrt)
            for b in (1, 3):
                act.wait_ge(sums_done, b + 1)
                a.activation(agg[:, b * SB_COLS:(b + 1) * SB_COLS], sums_ps[b][:, 0:SB_COLS], ACT.Copy).then_inc(agg_ready, 1)
            for q in range(len(CHUNKS) + 1):
                if q < len(CHUNKS):
                    lo, hi = CHUNKS[q]
                    act.wait_ge(y_ready, q + 1)
                    a.activation(sq[0:USED, :, lo:hi, :], y[0:USED, :, lo:hi, :], ACT.Square).then_inc(squared, 1)
                if q:
                    lo, hi = CHUNKS[q - 1]
                    act.wait_ge(y_var, q)
                    a.activation(std[0:USED, :, lo:hi], var[0:USED, :, lo:hi], ACT.Sqrt, bias=eps[0:USED, 0:1],
                                 scale=1.0 / C).then_inc(y_std, 1)

        @block.tensor
        def _(pe):
            m = nc.tensor
            pe.wait_ge(s_ident, 2)
            for j in range(BLK):
                if j % 4 == 0:
                    pe.wait_ge(s_pairs, j // 4 + 1)
                last = m.transpose(bank[j // 4][:, (j % 4) * USED:(j % 4 + 1) * USED],
                                   x_pairs[0:USED, j, :, :].rearrange("p h c -> p (h c)"), ident[0:USED, 0:USED])
                if j % 4 == 3 or j == BLK - 1:
                    last.then_inc(s_xt, 1)
            pe.wait_ge(s_w, 16 * 2)
            for b, (lo, hi) in enumerate(CHUNKS):
                pe.wait_ge(s_xc, b + 1)
                m.matmul(bank[4 + b][:, 0:(hi - lo) * USED], w_diag[:, :, :].rearrange("p h c -> p (h c)"),
                         x_turned[:, lo * USED:hi * USED], start=True, stop=True).then_inc(s_p1, 1)
                if b == 1:
                    pe.wait_ge(s_base, 1)
                    pe.wait_ge(s_xc, len(CHUNKS))
                    m.matmul(bank[3][:, BASE:BASE + PAIRS], ones[0:1, :], base_row[:, :], start=True, stop=True).then_inc(s_base_ps, 1)
            pe.wait_ge(s_w1, 16 * 3)
            for i, ready in enumerate((s_a_ps, s_b_ps)):
                for j in range(BLK):
                    pe.wait_ge(s_th, j // 4 + 1 if i == 0 else len(CHUNKS))
                    if i == 0 and j == BLK - 1:
                        pe.wait_ge(s_outside, 1)
                    last = m.matmul(bank[4 * i + j // 4][0:USED, (j % 4) * P:(j % 4 + 1) * P],
                                    p1_turned[:, j * USED:(j + 1) * USED],
                                    w1_diag[:, i, :, :].rearrange("p h c -> p (h c)"), start=True, stop=True)
                    if i == 0 and j == BLK - 1:
                        last = m.matmul(bank[3][0:1, BASE:BASE + GROUPS], ones[:, 0:1], outside_n[:, :], start=True, stop=True)
                    if j % 4 == 3 or j == BLK - 1:
                        last.then_inc(ready, 1)
            pe.wait_ge(s_w2, 16 * 2)
            pe.wait_ge(s_a, 2)
            w2_b = w2_sb[:, :].rearrange("k (j b) -> k b j", b=NB)
            for b in range(NB):
                last = m.transpose(bank[0][0:H, b * H:(b + 1) * H], w2_b[:, b, :], ident[0:H, 0:H])
            last.then_inc(s_w2t, 1)
            pe.wait_ge(s_w2c, 1)
            for b in range(NB):
                last = m.matmul(bank[1][:, b * C:(b + 1) * C], w2_turned[:, b, :, :].rearrange("j d k -> j (d k)"),
                                iiw_sb[:, :], start=True, stop=True)
            last.then_inc(s_v, 1)
            pe.wait_ge(s_a, len(CHUNKS))
            pe.wait_ge(s_flags, 1)
            pe.wait_ge(s_v_out, 1)
            def keep_busy(n):
                for i in range(n):
                    m.matmul(sums_ps[i % 4][:, 0:SB_COLS], zeros[:, 0:P], zeros[:, 0:SB_COLS], start=False, stop=False,
                             skip_group_check=True)

            for b in range(4):
                m.matmul(sums_ps[b][:, 0:SB_COLS], zeros[:, 0:P], zeros[:, 0:SB_COLS], start=True, stop=False,
                         skip_group_check=True)
            keep_busy(20)
            pe.wait_ge(s_vc, 1)
            pe.wait_ge(s_b, len(CHUNKS))

            def transpose_h(g, slot):
                pe.wait_ge(h_ready, g + 1)
                for t in range(TG):
                    last = m.transpose(turn_ps[slot][:, t * P // 2:(t + 1) * P // 2].bitcast(F16),
                                       h_parts[:, slot, t, :, :].rearrange("p a k -> p (a k)"), ident16[:, :])
                last.then_inc(h_transposed, 1)

            def times_v(g, slot, t, first):
                if t == 0:
                    pe.wait_ge(h_copied, g + 1)
                if t == DVE_TILE + 2:
                    pe.wait_ge(dve_products, g + 1)
                elif t == 2:
                    pe.wait_ge(act_products, TA * g + 1)
                elif not first:
                    pe.wait_ge(act_products, TA * g + t - 1)
                for part in range(2):
                    last = m.matmul(hv_ps[t % 2][:, :], h_turned[:, slot, t, :], v_parts[:, part, :],
                                    start=(part == 0), stop=(part == 1))
                last.then_inc(hv_ready, 1)

            def scatter_tile(g, slot, t, close=False):
                if t == 0:
                    pe.wait_ge(parts_ready, g + 1)
                pe.wait_ge(onehot_ready, TG * g + t + 1)
                for part, b in [(p, b) for b in range(4) for p in range(2)] if close else [(p, b) for p in range(2) for b in range(4)]:
                    last = m.matmul(sums_ps[b][:, 0:SB_COLS],
                                    parts[:, slot, t, part, :, :].rearrange("p h c -> p (h c)"),
                                    onehot[:, slot, t, b * SB_COLS:(b + 1) * SB_COLS],
                                    start=False, stop=close and part == 1, skip_group_check=True)
                    if close and part == 1:
                        last.then_inc(sums_done, 1)
                if not close:
                    last.then_inc(scattered, 1)

            def window_rows(g, pair, slot):
                pe.wait_ge(win_hot_ready, pair + 1)
                pe.wait_ge(win_rows_loaded, 16 * (pair + 1))
                for t in range(TG):
                    for part in range(2):
                        last = m.matmul(turn_ps[slot][:, WIN + t * H:WIN + (t + 1) * H], win_hot[:, :, TG * slot + t],
                                        win_rows[:, part, :], start=(part == 0), stop=(part == 1))
                last.then_inc(windowed, 1)

            def group(g, pair, slot, first=False, back=True, more=True):
                transpose_h(g, slot)
                for t in range(TG):
                    if back and t != 1:
                        scatter_tile(g - 2, slot, max(t - 1, 0))
                    times_v(g, slot, t, first)
                    if t == 1 and more:
                        window_rows(g + 1, pair + slot, 1 - slot)
                if back:
                    scatter_tile(g - 2, slot, TG - 1)

            window_rows(0, 0, 0)
            for g in range(4):
                group(g, g // 2, g % 2, first=g == 0, back=g >= 2)
            with pe.Fori(2, PAIRS - 1) as i:
                for slot in range(2):
                    group(2 * i + slot, i, slot)
            for g in (GROUPS - 2, GROUPS - 1):
                group(g, PAIRS - 1, g % 2, more=g < GROUPS - 1)
            for g in range(GROUPS - 2, GROUPS):
                for t in range(TG):
                    scatter_tile(g, g % 2, t, close=(g, t) == (GROUPS - 1, TG - 1))

            pe.wait_ge(agg_ready, 4)
            pe.wait_ge(z_ready, GROUPS)
            pe.wait_ge(s_centre, 1)
            agg_by_block = agg[:, :].rearrange("p (n j) -> p j n", j=BLK)
            for j in range(BLK):
                last = m.matmul(bank[4 + j // 4][0:USED, (j % 4) * P:(j % 4 + 1) * P], agg_by_block[:, j, :],
                                centre[:, :], start=True, stop=True)
                if j % 4 == 3 or j == BLK - 1:
                    last.then_inc(agg_turned, 1)


_INS = ['x', 'src', 'dst', 'edge_attr_8', 'L0_gnn_pp_W', 'L0_gnn_pp_b', 'L0_gnn_pi_W1', 'L0_gnn_pi_b1',
        'L0_gnn_pi_W2', 'L0_gnn_ii_W', 'L0_gnn_ii_b']


def kernel(**inputs):
    import numpy as _np
    import concourse.bacc as _bacc
    from concourse import mybir as _mybir
    from concourse.bass_utils import run_bass_kernel_spmd as _run

    nc = _bacc.Bacc("TRN2", target_bir_lowering=False, num_devices=1)
    arrays, args = {}, []
    for name in _INS:
        a = _np.ascontiguousarray(inputs[name])
        arrays[f"in_{name}_dram"] = a
        args.append(nc.dram_tensor(f"in_{name}_dram", a.shape, _mybir.dt.from_np(a.dtype), kind="ExternalInput").ap())
    shape = inputs['x'].shape
    args.append(nc.dram_tensor("out_0_dram", tuple(shape), _mybir.dt.float32, kind="ExternalOutput").ap())
    gnn_residual_norm_kernel(nc, *args)
    r = _run(nc, [arrays], core_ids=[0])
    return r.results[0]["out_0_dram"]
```
